# Optimizing a Trainium2 kernel written in Bass

```python
import numpy as np
import jax
import jax.numpy as jnp

def _softmax(x, axis=-1):
    return jax.nn.softmax(x, axis=axis)

def _gelu(x):
    return jax.nn.gelu(x, approximate=True)

def _silu(x):
    return jax.nn.silu(x)

def _sigmoid(x):
    return jax.nn.sigmoid(x)

def _layernorm(x, axis=-1, eps=1e-05):
    m = jnp.mean(x, axis=axis, keepdims=True)
    v = jnp.var(x, axis=axis, keepdims=True)
    return (x - m) / jnp.sqrt(v + eps)

def _scatter_add(tgt, idx, src, axis=0):
    return tgt.at[idx].add(src)

def _segment_sum(src, seg, n):
    return jax.ops.segment_sum(src, seg, n)
kernel_name = 'mk_gnn_preln_d4_gnn_r8_470d09'

def setup_inputs(seed: int=0):
    np.random.seed(seed)
    _w = jnp.asarray

    def _rec_inputs():
        import jax
        import jax.numpy as jnp
        _gk = jax.random.key(seed)
        x = -0.000202 + 1 * jax.random.normal(jax.random.fold_in(_gk, 1), (6250, 128), jnp.float32)
        src = jax.random.randint(jax.random.fold_in(_gk, 2), (100000,), 0, 6250, jnp.int32)
        dst = jnp.minimum((6250 * jax.random.uniform(jax.random.fold_in(_gk, 3), (100000,)) ** 2.0).astype(jnp.int32), 49999)
        _o = jnp.argsort(dst, stable=True)
        src = src[_o]
        dst = dst[_o]
        edge_type_8 = jax.random.randint(jax.random.fold_in(_gk, 13), (100000,), 0, 8, jnp.int32)
        edge_weight = jax.random.uniform(jax.random.fold_in(_gk, 14), (100000,), jnp.float32, 0.0, 0.999998)
        edge_weight1 = jax.random.uniform(jax.random.fold_in(_gk, 15), (100000, 1), jnp.float32, 0.0, 0.999999)
        return (x, src, dst, edge_type_8, edge_weight, edge_weight1)
    x, src, dst, edge_type_8, edge_weight, edge_weight1 = _rec_inputs()

    def _L0_gnn_setup():
        import jax, jax.numpy as jnp
        import numpy as np
        N = 6250
        E = 100000
        H = 4
        D = 32
        IN = H * D
        key = jax.random.key(seed)
        ks = jax.random.split(key, 7)
        s = 0.1
        feature = jax.random.normal(ks[0], (N, IN), jnp.float32)
        Wq = jax.random.normal(ks[1], (H * D, IN), jnp.float32) * s
        Wk = jax.random.normal(ks[2], (H * D, IN), jnp.float32) * s
        Wv = jax.random.normal(ks[3], (H * D, IN), jnp.float32) * s
        Wscale = jax.random.normal(ks[4], (IN * H, H * D), jnp.float32) * s
        src = jax.random.randint(ks[5], (E,), 0, N)
        dst = jax.random.randint(ks[6], (E,), 0, N)
        return {'feature': feature, 'Wq': Wq, 'Wk': Wk, 'Wv': Wv, 'Wscale': Wscale, 'src': src, 'dst': dst}
    _L0_gnn_all = _L0_gnn_setup()
    _L0_gnn_in = {k: v for k, v in _L0_gnn_all.items() if k in ('Wq', 'Wk', 'Wv', 'Wscale')}
    del _L0_gnn_all

    def _L1_gnn_setup():
        import jax, jax.numpy as jnp
        import numpy as np
        N_NODES = 12500
        N_EDGES = 125000
        EMB_DIM = 128
        NEG_SLOPE = 0.01
        key = jax.random.key(seed)
        k1, k2, k3, k4 = jax.random.split(key, 4)
        x = jax.random.normal(k1, (N_NODES, EMB_DIM), dtype=jnp.float32)
        edge_index = jax.random.randint(k2, (2, N_EDGES), 0, N_NODES, dtype=jnp.int64)
        edge_attrs = jax.random.uniform(k3, (N_EDGES,), dtype=jnp.float32)
        limit = float(np.sqrt(6.0 / (EMB_DIM + EMB_DIM)))
        W1_w = jax.random.uniform(k4, (EMB_DIM, EMB_DIM), dtype=jnp.float32, minval=-limit, maxval=limit)
        W1_b = jnp.zeros((EMB_DIM,), dtype=jnp.float32)
        return {'x': x, 'edge_index': edge_index, 'edge_attrs': edge_attrs, 'W1_w': W1_w, 'W1_b': W1_b}
    _L1_gnn_all = _L1_gnn_setup()
    _L1_gnn_in = {k: v for k, v in _L1_gnn_all.items() if k in ('W1_w', 'W1_b')}
    del _L1_gnn_all

    def _L2_gnn_setup():
        import jax, jax.numpy as jnp
        import numpy as np
        N_NODES = 12500
        N_EDGES = 75000
        FEAT = 128
        N_RELS = 8
        key = jax.random.key(seed)
        k1, k2, k3, k4, k5, k6, k7 = jax.random.split(key, 7)
        return {'h': jax.random.normal(k1, (N_NODES, FEAT), dtype=jnp.float32), 'weight': jax.random.normal(k2, (N_RELS, FEAT, FEAT), dtype=jnp.float32) * (1.0 / np.sqrt(FEAT)), 'gate_weight': jax.random.normal(k3, (N_RELS, FEAT, 1), dtype=jnp.float32) * (1.0 / np.sqrt(FEAT)), 'norm': jax.random.uniform(k4, (N_EDGES, 1), dtype=jnp.float32), 'src': jax.random.randint(k5, (N_EDGES,), 0, N_NODES, dtype=jnp.int32), 'dst': jax.random.randint(k6, (N_EDGES,), 0, N_NODES, dtype=jnp.int32), 'rel_type': jax.random.randint(k7, (N_EDGES,), 0, N_RELS, dtype=jnp.int32)}
    _L2_gnn_all = _L2_gnn_setup()
    _L2_gnn_in = {k: v for k, v in _L2_gnn_all.items() if k in ('weight', 'gate_weight')}
    del _L2_gnn_all

    def _L3_gnn_setup():
        import jax, jax.numpy as jnp
        import numpy as np
        N_NODES = 6250
        N_EDGES = 80000
        D_FEAT = 128
        NUM_RELS = 8
        EPS = 0.0
        key = jax.random.key(seed)
        k_feat, k_w, k_et, k_src, k_dst = jax.random.split(key, 5)
        feat = jax.random.normal(k_feat, (N_NODES, D_FEAT), dtype=jnp.float32)
        W = jax.random.normal(k_w, (NUM_RELS, D_FEAT, D_FEAT), dtype=jnp.float32) * 0.05
        etypes = jax.random.randint(k_et, (N_EDGES,), 0, NUM_RELS, dtype=jnp.int32)
        src = jax.random.randint(k_src, (N_EDGES,), 0, N_NODES, dtype=jnp.int32)
        dst = jax.random.randint(k_dst, (N_EDGES,), 0, N_NODES, dtype=jnp.int32)
        return {'feat': feat, 'W': W, 'etypes': etypes, 'src': src, 'dst': dst}
    _L3_gnn_all = _L3_gnn_setup()
    _L3_gnn_in = {k: v for k, v in _L3_gnn_all.items() if k in ('W',)}
    del _L3_gnn_all
    return {'x': x, 'src': src, 'dst': dst, 'edge_type_8': edge_type_8, 'edge_weight': edge_weight, 'edge_weight1': edge_weight1, 'L0_gnn_Wq': _L0_gnn_in['Wq'], 'L0_gnn_Wk': _L0_gnn_in['Wk'], 'L0_gnn_Wv': _L0_gnn_in['Wv'], 'L0_gnn_Wscale': _L0_gnn_in['Wscale'], 'L1_gnn_W1_w': _L1_gnn_in['W1_w'], 'L1_gnn_W1_b': _L1_gnn_in['W1_b'], 'L2_gnn_weight': _L2_gnn_in['weight'], 'L2_gnn_gate_weight': _L2_gnn_in['gate_weight'], 'L3_gnn_W': _L3_gnn_in['W']}

def reference(x, src, dst, edge_type_8, edge_weight, edge_weight1, L0_gnn_Wq, L0_gnn_Wk, L0_gnn_Wv, L0_gnn_Wscale, L1_gnn_W1_w, L1_gnn_W1_b, L2_gnn_weight, L2_gnn_gate_weight, L3_gnn_W):
    import jax
    import jax.numpy as jnp

    def _L0_gnn_ref(feature, Wq, Wk, Wv, Wscale, src, dst):
        import jax, jax.numpy as jnp
        import numpy as np
        N = 6250
        E = 100000
        H = 4
        D = 32
        IN = H * D
        q = (feature @ Wq.T).reshape(N, H, D)
        k = (feature @ Wk.T).reshape(N, H, D)
        v = (feature @ Wv.T).reshape(N, H, D)
        scores = jnp.einsum('ehd,ehd->eh', q[src], k[dst]) * D ** (-0.5)
        mx = jax.ops.segment_max(scores, dst, num_segments=N)
        ex = jnp.exp(scores - mx[dst])
        den = jax.ops.segment_sum(ex, dst, num_segments=N)
        a = ex / den[dst]
        msg = v[src] * a[:, :, None]
        ft = jax.ops.segment_sum(msg, dst, num_segments=N)
        rst = (ft.reshape(N, H * D) @ Wscale.T).reshape(N, H, IN)
        return rst.sum(axis=1) + feature

    def _L1_gnn_ref(x, edge_index, edge_attrs, W1_w, W1_b):
        import jax, jax.numpy as jnp
        import numpy as np
        N_NODES = 12500
        N_EDGES = 125000
        EMB_DIM = 128
        NEG_SLOPE = 0.01
        n = x.shape[0]
        from_, to_ = (edge_index[0], edge_index[1])
        deg = jax.ops.segment_sum(jnp.ones((to_.shape[0],), dtype=x.dtype), to_, num_segments=n)
        deg_inv = jnp.where(deg > 0, 1.0 / jnp.sqrt(deg), 0.0)
        norm = deg_inv[from_] * deg_inv[to_]
        x_i = x[from_]
        x_j = x[to_]
        m_j = norm[:, None] * (x_j + x_j * x_i @ W1_w.T + W1_b)
        out = jax.ops.segment_sum(m_j, to_, num_segments=n)
        out = jnp.where(out >= 0, out, NEG_SLOPE * out)
        return out

    def _L2_gnn_ref(h, weight, gate_weight, norm, src, dst, rel_type):
        import jax, jax.numpy as jnp
        import numpy as np
        N_NODES = 12500
        N_EDGES = 75000
        FEAT = 128
        N_RELS = 8
        h_all = jnp.einsum('nd,rdf->nrf', h, weight)
        gate_all = jnp.einsum('nd,rdo->nro', h, gate_weight)[..., 0]
        msg = h_all[src, rel_type] * norm
        gate = jax.nn.sigmoid(gate_all[src, rel_type])[:, None]
        msg = msg * gate
        out = jax.ops.segment_sum(msg, dst, num_segments=h.shape[0])
        return jax.nn.relu(out)

    def _L3_gnn_ref(feat, W, etypes, src, dst):
        import jax, jax.numpy as jnp
        import numpy as np
        N_NODES = 6250
        N_EDGES = 80000
        D_FEAT = 128
        NUM_RELS = 8
        EPS = 0.0
        n_nodes = feat.shape[0]
        num_rels = W.shape[0]
        x = feat[src]
        m = jnp.zeros_like(x)
        for r in range(num_rels):
            mask = (etypes == r)[:, None]
            m = m + jnp.where(mask, x, 0.0) @ W[r]
        neigh = jax.ops.segment_sum(m, dst, num_segments=n_nodes)
        return (1.0 + EPS) * feat + neigh
    edge_index = jnp.stack([src, dst])
    h = jnp.maximum(_layernorm(x, axis=-1), 0.0)
    x = x + _L0_gnn_ref(h, L0_gnn_Wq, L0_gnn_Wk, L0_gnn_Wv, L0_gnn_Wscale, src, dst)
    h = jnp.maximum(_layernorm(x, axis=-1), 0.0)
    x = x + _L1_gnn_ref(h, edge_index, edge_weight, L1_gnn_W1_w, L1_gnn_W1_b)
    h = jnp.maximum(_layernorm(x, axis=-1), 0.0)
    x = x + _L2_gnn_ref(h, L2_gnn_weight, L2_gnn_gate_weight, edge_weight1, src, dst, edge_type_8)
    h = jnp.maximum(_layernorm(x, axis=-1), 0.0)
    x = x + _L3_gnn_ref(h, L3_gnn_W, edge_type_8, src, dst)
    return x

_drawn_inputs = setup_inputs


def setup_inputs(seed=0):
    import zlib

    import numpy as np

    out = dict(_drawn_inputs(seed))
    spreads = {'L1_gnn_W1_b': (0.0, 0.1)}
    factors = {}
    for name, (base, spread) in spreads.items():
        noise = np.random.default_rng([zlib.crc32(name.encode()), seed]).standard_normal(out[name].shape)
        drawn = base * np.exp(spread * noise) if base else spread * noise
        out[name] = jnp.asarray(drawn.astype(out[name].dtype))
    for name, factor in factors.items():
        out[name] = (out[name] * factor).astype(out[name].dtype)
    return out
```

```python
from contextlib import ExitStack

import concourse.bass as bass
from concourse import mybir

P = 128
N, E, F = 6250, 100000, 128
HEADS, HDIM = 4, 32
RELS = 8
EPS = 1e-5
SLOPE = 0.01

NODE_TILES = -(-N // P)
NPAD = NODE_TILES * P
NTAIL = N - (NODE_TILES - 1) * P
EDGE_TILES = -(-E // P)
ETAIL = E - (EDGE_TILES - 1) * P
EXTRA = NODE_TILES - 1
STEPS = EDGE_TILES + EXTRA
CHUNKS = -(-EDGE_TILES // P)
CTAIL = EDGE_TILES - (CHUNKS - 1) * P

GROUPS = P // HEADS
BLOCKS = -(-EDGE_TILES // GROUPS)
ROW = BLOCKS * P

RING = 4
LAG = 2
VRING = 3
UNROLL2 = VRING * RING

NO_NODE = 1 << 20
LOWEST = -3.0e38
ACCW = F + HEADS + 1

F32 = mybir.dt.float32
I32 = mybir.dt.int32
ALU = mybir.AluOpType
ACT = mybir.ActivationFunctionType
AX = mybir.AxisListType


def at_least(eng, sem, value):
    if isinstance(value, int) and value <= 0:
        return
    eng.wait_ge(sem, value)


def rolled(eng, start, stop, unroll, body):
    first = max(unroll, -(-start // unroll) * unroll)
    rounds = stop // unroll
    for s in range(start, min(first, stop)):
        body(s, s % unroll, s // unroll)
    if rounds > first // unroll:
        with eng.Fori(first // unroll, rounds) as r:
            for k in range(unroll):
                body(r * unroll + k, k, r)
    for s in range(max(first, rounds * unroll), stop):
        body(s, s % unroll, s // unroll)


def graph_layers(nc, x, src, dst, rel, weight1, Wq, Wk, Wv, Wscale, W1, b1, W2, gate2, W3, out):
    ctx = ExitStack()
    with ctx:
        def sb(name, shape, dt=F32):
            return ctx.enter_context(nc.sbuf_tensor(name, shape, dt))

        def sem(name):
            return ctx.enter_context(nc.semaphore(name))

        def sems(name, n):
            return [sem(f"{name}{i}") for i in range(n)]

        def dram(name, shape, dt=F32):
            return nc.dram_tensor(name, shape, dt).ap()

        win_d = dram("win_d", (STEPS,), I32)
        tile_d = dram("tile_d", (EXTRA,), I32)
        rows_d = dram("rows_d", (EDGE_TILES, 4 * P))
        dst_d = dram("dst_d", (GROUPS * ROW + 2,), I32)
        qv_d = dram("qv_d", (NPAD, 2 * F))
        v_d = dram("v_d", (P, STEPS, F))
        t1_d = dram("t1_d", (NPAD, F + 1))
        t2_d = dram("t2_d", (NPAD * RELS, F))
        t3_d = dram("t3_d", (NPAD * RELS, F))

        X = sb("X", [P, NODE_TILES, F])
        H = sb("H", [P, NODE_TILES, F])
        SUMS = sb("SUMS", [P, NODE_TILES, ACCW])
        big = sb("big", [P, 2 * ROW])
        rows = sb("rows", [P, 2 * (ROW + 2)])
        col = sb("col", [P, 4, STEPS])
        SW = sb("SW", [P, STEPS, HEADS + 1])
        ring = sb("ring", [P, RING, 2 * F])
        idx = sb("idx", [P, RING], I32)
        onehot = sb("onehot", [P, RING, P])
        onehotT = sb("onehotT", [P, RING, P])
        prod = sb("prod", [P, 2, F])
        vin = sb("vin", [P, VRING, RING, F])
        vw = sb("vw", [P, RING, ACCW])
        hs = sb("hs", [P, 2, F])
        hT = sb("hT", [P, 2, F])
        wraw = sb("wraw", [P, 4, F])
        wsraw = sb("wsraw", [P, HEADS, F])
        wqkvT = sb("wqkvT", [P, 3 * F])
        wsT = sb("wsT", [P, F])
        w1T = sb("w1T", [P, F])
        w2 = sb("w2", [P, RELS, F])
        w3 = sb("w3", [P, RELS, F])
        g2 = sb("g2", [P, RELS])
        bias = sb("bias", [P, F])
        iota_row = sb("iota_row", [P, P])
        iota_col = sb("iota_col", [P, 1])
        next_row = sb("next_row", [P, EXTRA])
        next_col = sb("next_col", [P, 1])
        ident = sb("ident", [P, P])
        one = sb("one", [1, 2])
        win = sb("win", [1, STEPS], I32)
        tile = sb("tile", [1, EXTRA], I32)
        ends = sb("ends", [P, CHUNKS], I32)
        few = sb("few", [P, 8], I32)
        fewf = sb("fewf", [P, 8])
        xrows = sb("xrows", [P, 4 * P])
        stats = sb("stats", [P, NODE_TILES, 6])
        ln = sb("ln", [P, 4, NODE_TILES])
        rstd = sb("rstd", [P, NODE_TILES])
        shift = sb("shift", [P, NODE_TILES])
        rden = sb("rden", [P, NODE_TILES, HEADS])
        dinv = sb("dinv", [P, NODE_TILES])
        dtmp = sb("dtmp", [P, 2, NODE_TILES])
        carry = sb("carry", [P, 4])
        crow = sb("crow", [1, 4, P + 1])
        y = sb("y", [P, 2, F])
        hb = sb("hb", [P, 2, F])
        gate = sb("gate", [P, 2, 2, RELS])
        minus1 = sb("minus1", [1, 4], I32)

        K = big[:, 0:NODE_TILES * F].rearrange("p (t f) -> p t f", f=F)
        ST = big[:, 0:ROW]
        FT = big[:, ROW:2 * ROW]
        RI = rows[:, 0:CHUNKS * 3 * P].bitcast(I32).rearrange("p (c k i) -> p c k i", c=CHUNKS, k=3)
        R = big[:, 0:CHUNKS * 4 * P].rearrange("p (c k i) -> p c k i", c=CHUNKS, k=4)
        spare = rows[:, CHUNKS * 3 * P:CHUNKS * 3 * P + 3 * EDGE_TILES].rearrange("p (k e) -> p k e", k=3)
        winb_i = spare[:, 0, :].bitcast(I32)
        winb = spare[:, 1, :]
        below = spare[:, 2, :]
        Tst = big[:, 0:NODE_TILES * (F + 1)].rearrange("p (t f) -> p t f", f=F + 1)
        drow = rows[:, 0:ROW + 2].bitcast(I32)
        MT = rows[:, 0:ROW]
        pen = rows[:, ROW + 2:2 * ROW + 2]
        stage = rows[:, ROW + 2:ROW + 2 + 2 * RELS * F].rearrange("p (k f) -> p k f", k=2)

        ps = [ctx.enter_context(nc.psum_tensor(f"ps{i}", [P, 512], F32)) for i in range(8)]

        s_const = sem("s_const")
        s_edges = sem("s_edges")
        s_x = sem("s_x")
        s_w = sem("s_w")
        s_scratch = sem("s_scratch")
        s_extra = sem("s_extra")
        dve_step = sem("dve_step")
        act_step = sem("act_step")
        pe_prep = sem("pe_prep")
        s_dpad = sem("s_dpad")
        s_drow = sem("s_drow")
        s_out = sem("s_out")
        s_mid_pe = sem("s_mid_pe")
        s_mid_cp = sem("s_mid_cp")
        s_back_pe = sem("s_back_pe")
        s_back_cp = sem("s_back_cp")
        s_fold = sem("s_fold")

        q0 = dict(idx=sem("q0_idx"), issued=sem("q0_issued"), rows=sems("q0_rows", RING), onehot=sem("q0_onehot"),
                             turned=sem("q0_turned"), copied=sem("q0_copied"), kexp=sem("q0_kexp"),
                             prod=sem("q0_prod"), score=sem("q0_score"), saved=sems("q0_saved", RING))
        a0 = dict(loaded=sems("a0_loaded", VRING), vw=sem("a0_vw"), wcol=sem("a0_wcol"),
                             onehot=sem("a0_onehot"), summed=sem("a0_summed"), added=sem("a0_added"))

        def gsems(name):
            return dict(idx=sem(name + "_idx"), issued=sem(name + "_issued"), rows=sems(name + "_rows", RING),
                                   onehot=sem(name + "_onehot"), summed=sem(name + "_summed"),
                                   added=sem(name + "_added"), zero=sem(name + "_zero"))

        g1, gr2, gr3 = gsems("g1"), gsems("g2"), gsems("g3")

        def dsems(name, *more):
            s = {k: sem(f"{name}_{k}") for k in more}
            s["stored"] = sems(name + "_stored", 2)
            return s

        d0 = dsems("d0", "ln", "h", "xadd", "turned", "hT", "prod", "qv", "k")
        d2 = dsems("d2", "ln", "h", "turned", "hT", "gate", "gexp", "gone", "gsig", "prod", "dve", "act")
        d3 = dsems("d3", "ln", "h", "xadd", "turned", "hT", "prod", "dve", "act")
        p0 = dsems("p0", "inn", "turned", "T", "prod", "x", "stats")
        p1 = dsems("p1", "inn", "turned", "T", "prod", "hb", "y", "z", "x", "stats")
        p2 = dsems("p2", "stats")
        ln0 = dsems("ln0", "stats")
        s_t1 = sem("s_t1")
        s_t1d = sem("s_t1d")
        s_lnsq = sem("s_lnsq")
        s_dq = sem("s_dq")
        s_h1 = sem("s_h1")

        block = ctx.enter_context(nc.Block())

        mark = {}

        @block.vector
        def _(v):
            count = [0]

            def link(ins, name=None):
                count[0] += 1
                ins.then_inc(dve_step, 1)
                v.wait_ge(dve_step, count[0])
                if name:
                    mark[name] = count[0]

            win_regs = [v.alloc_register(f"win{k}") for k in range(RING)]
            tile_regs = [v.alloc_register(f"tile{k}") for k in range(RING)]

            def windows(s, n):
                v.reg_load(win_regs[0:n], win[0:1, bass.ds(s, n)])
                return [v.snap(r, min_val=0, max_val=NODE_TILES - 1) for r in win_regs[0:n]]

            def edge_tiles(s, n):
                v.reg_load(tile_regs[0:n], tile[0:1, bass.ds(s, n)])
                return [v.snap(r, min_val=0, max_val=EDGE_TILES - 1) for r in tile_regs[0:n]]

            v.wait_ge(s_const, 1)
            link(v.tensor_scalar(ident[:], iota_row[:], iota_col[:, 0:1], None, ALU.is_equal), "ident")
            v.wait_ge(s_edges, 12 * 16)
            link(v.tensor_scalar(ends[:], RI[:, :, 0, P - 1], 7, None, ALU.arith_shift_right), "ends")
            link(v.tensor_copy(R[:, :, 0:2, :], RI[:, :, 0:2, :]))
            link(v.scalar_tensor_tensor(R[:, :, 2, :], RI[:, :, 1, :], float(RELS), RI[:, :, 2, :],
                                        ALU.mult, ALU.add), "rows")
            v.wait_ge(s_scratch, 16 * 8)
            link(v.tensor_copy(winb[:], winb_i[:]))
            link(v.tensor_scalar(below[0:EXTRA, 0:EDGE_TILES - 1], winb[0:EXTRA, 1:EDGE_TILES],
                                 next_col[0:EXTRA, 0:1], None, ALU.is_lt))
            link(v.tensor_reduce(fewf[0:EXTRA, 0:1], below[0:EXTRA, 0:EDGE_TILES - 1], AX.X, ALU.add))
            link(v.tensor_copy(few[0:EXTRA, 0:1], fewf[0:EXTRA, 0:1]), "tiles")
            for c in range(CHUNKS + 1):
                w = P if c < CHUNKS - 1 else CTAIL if c == CHUNKS - 1 else EXTRA
                v.wait_ge(pe_prep, c + 1)
                o = c * P if c < CHUNKS else EDGE_TILES
                link(v.tensor_copy(col[:, :, o:o + w],
                                   ps[c][:].rearrange("p (k i) -> p k i", k=4)[:, :, 0:w]), f"col{c}")
            link(v.scalar_tensor_tensor(col[:, 0, 0:EDGE_TILES], winb[:], -float(P), col[:, 0, 0:EDGE_TILES],
                                        ALU.mult, ALU.add))
            link(v.scalar_tensor_tensor(col[:, 0, EDGE_TILES:STEPS], next_row[:], -float(P),
                                        col[:, 0, EDGE_TILES:STEPS], ALU.mult, ALU.add), "cols")
            v.wait_ge(s_w, 16 * 9)
            link(v.tensor_reduce(hs[:, 0, :], wsraw[:].rearrange("p h c -> p c h"), AX.X, ALU.add), "wsum")
            v.wait_ge(pe_prep, CHUNKS + 2)
            link(v.tensor_scalar(wqkvT[:, 0:F], ps[0][:, 0:F], HDIM ** -0.5, None, ALU.mult))
            link(v.tensor_copy(wqkvT[:, F:2 * F], ps[0][:, 2 * F:3 * F]))
            link(v.tensor_copy(wqkvT[:, 2 * F:3 * F], ps[0][:, F:2 * F]))
            link(v.tensor_copy(w1T[:], ps[0][:, 3 * F:4 * F]))
            link(v.tensor_copy(wsT[:], ps[1][:, 0:F]), "weights")

            def norm_stats(done):
                me, qe, mo, qo = (stats[:, :, j] for j in (1, 2, 4, 5))
                v.wait_ge(done, NODE_TILES)
                link(v.tensor_tensor(ln[:, 0, :], me, mo, ALU.add))
                link(v.tensor_tensor(ln[:, 1, :], me, mo, ALU.subtract))
                link(v.tensor_tensor(ln[:, 2, :], qe, qo, ALU.add))
                link(v.tensor_tensor(ln[:, 1, :], ln[:, 1, :], ln[:, 1, :], ALU.mult))
                link(v.tensor_scalar(ln[:, 2, :], ln[:, 2, :], 1.0 / F, EPS, ALU.mult, ALU.add))
                link(v.scalar_tensor_tensor(ln[:, 3, :], ln[:, 1, :], 0.25, ln[:, 2, :], ALU.mult, ALU.add),
                     f"var{len([m for m in mark if m.startswith('var')])}")

            def norm_scale(n):
                v.wait_ge(s_lnsq, n + 1)
                link(v.reciprocal(rstd[:], ln[:, 3, :]))
                link(v.scalar_tensor_tensor(shift[:], ln[:, 0, :], -0.5, rstd[:], ALU.mult, ALU.mult), f"ln{n}")

            v.wait_ge(s_x, 32)
            rolled(v, 0, NODE_TILES, 4, lambda s, k, r: v.bn_stats(
                stats[:, bass.ds(s, 1), :], X[:, bass.ds(s, 1), :]).then_inc(ln0["stats"], 1))
            norm_stats(ln0["stats"])
            norm_scale(0)

            def hT_copy(sems_, s, k):
                v.wait_ge(sems_["turned"], s + 1)
                at_least(v, sems_["prod"], s - 1)
                v.tensor_copy(hT[:, k, :], ps[k][:, 0:F]).then_inc(sems_["hT"], 1)

            def d0_tile(s, k, r):
                hT_copy(d0, s, k)
                v.wait_ge(d0["prod"], s + 1)
                v.tensor_copy(K[:, bass.ds(s, 1), :],
                              ps[4 + k][:, 0:F].rearrange("p (a f) -> p a f", a=1)).then_inc(d0["k"], 1)

            rolled(v, 0, NODE_TILES, 2, d0_tile)

            def build(s, k, done, value, sig, weighted=False):
                at_least(v, done, value)
                v.tensor_scalar(onehot[:, k, :], iota_row[:], col[:, 0, bass.ds(s, 1)],
                                col[:, 3, bass.ds(s, 1)] if weighted else None, ALU.is_equal,
                                **({"op1": ALU.mult} if weighted else {})).then_inc(sig, 1)

            v.wait_ge(d0["k"], NODE_TILES)

            def score(s, k, r):
                if not (isinstance(s, int) and s + LAG >= STEPS):
                    build(s + LAG, (k + LAG) % RING, q0["turned"], s + LAG - RING + 1, q0["onehot"])
                v.wait_ge(q0["rows"][k], 16 * (r + 1))
                v.wait_ge(q0["kexp"], s + 1)
                at_least(v, q0["score"], s - 1)
                v.tensor_tensor(prod[:, k % 2, :], ring[:, k, 0:F], ps[4 + k][:, 0:F],
                                ALU.mult).then_inc(q0["prod"], 1)
                v.wait_ge(q0["prod"], s + 1)
                v.tensor_reduce(SW[:, bass.ds(s, 1), 0:HEADS],
                                prod[:, k % 2, :].rearrange("p (a h d) -> p a h d", a=1, h=HEADS),
                                AX.X, ALU.add).then_inc(q0["score"], 1)

            for s in range(LAG):
                build(s, s, None, 0, q0["onehot"])
            rounds = STEPS // RING
            for s in range(RING):
                score(s, s, 0)
            with v.Fori(1, rounds) as r:
                for k in range(RING):
                    score(r * RING + k, k, r)
            for s in range(rounds * RING, STEPS):
                score(s, s % RING, rounds)
            v.wait_ge(q0["score"], STEPS)

            def fold(s, e, j):
                at_least(v, s_fold, s)
                v.tensor_tensor(SW[:, bass.ds(e, 1), 0:HEADS], SW[:, bass.ds(e, 1), 0:HEADS],
                                SW[:, bass.ds(s + EDGE_TILES, 1), 0:HEADS], ALU.add).then_inc(s_fold, 1)

            v.wait_ge(s_scratch, 16 * 10)
            e = edge_tiles(0, RING)
            for k in range(RING):
                fold(k, e[k], k)
            with v.Fori(1, EXTRA // RING) as r:
                e = edge_tiles(r * RING, RING)
                for k in range(RING):
                    fold(r * RING + k, e[k], k)

            SWt = SW[:, 0:GROUPS * BLOCKS, 0:HEADS].rearrange("p (g b) h -> p b h g", b=BLOCKS)
            v.wait_ge(s_fold, EXTRA)
            link(v.tensor_copy(FT.rearrange("p (b h g) -> p b h g", b=BLOCKS, h=HEADS), SWt), "blocks")
            for b in range(0, BLOCKS, 4):
                n = min(4, BLOCKS - b)
                v.wait_ge(s_mid_pe, b // 4 + 1)
                v.tensor_copy(ST[:, b * P:(b + n) * P], ps[(b // 4) % 2][:, 0:n * P]).then_inc(s_mid_cp, 1)
            v.wait_ge(s_mid_cp, -(-BLOCKS // 4))
            v.wait_ge(s_drow, 64)
            link(v.tensor_tensor(pen[:], drow[:, 1:ROW + 1], drow[:, 0:ROW], ALU.not_equal))
            link(v.tensor_scalar(pen[:], pen[:], LOWEST, None, ALU.mult))
            link(v.tensor_tensor_scan(FT, pen, ST, LOWEST, ALU.add, ALU.max))
            link(v.tensor_tensor(carry[:, 0:1], drow[:, ROW:ROW + 1], drow[:, 0:1], ALU.not_equal))
            link(v.tensor_scalar(carry[:, 1:2], carry[:, 0:1], LOWEST, None, ALU.mult))
            link(v.tensor_copy(carry[:, 0:1], FT[:, ROW - 1:ROW]), "carry_f")
            v.wait_ge(s_mid_pe, -(-BLOCKS // 4) + 1)
            link(v.tensor_copy(crow[:, 0:2, 1:P + 1], ps[2][0:1, 0:2 * P].rearrange("p (k i) -> p k i", k=2)))
            link(v.tensor_tensor_scan(crow[:, 2, 1:P + 1], crow[:, 1, 1:P + 1], crow[:, 0, 1:P + 1],
                                      LOWEST, ALU.add, ALU.max))
            link(v.memset(crow[:, 2, 0:1], LOWEST), "crow_f")
            v.wait_ge(s_mid_pe, -(-BLOCKS // 4) + 2)
            link(v.tensor_copy(carry[:, 2:3], ps[3][:, 0:1]))
            link(v.tensor_tensor_scan(FT, pen, ST, carry[:, 2:3], ALU.add, ALU.max))
            link(v.tensor_tensor(pen[:], drow[:, 1:ROW + 1], drow[:, 2:ROW + 2], ALU.not_equal))
            link(v.tensor_scalar(pen[:], pen[:], LOWEST, None, ALU.mult))
            link(v.tensor_tensor(carry[:, 0:1], drow[:, 1:2], drow[:, ROW + 1:ROW + 2], ALU.not_equal))
            link(v.tensor_scalar(carry[:, 1:2], carry[:, 0:1], LOWEST, None, ALU.mult))
            link(v.tensor_tensor_scan(MT[:, ::-1], pen[:, ::-1], FT[:, ::-1], LOWEST, ALU.add, ALU.max))
            link(v.tensor_copy(carry[:, 0:1], MT[:, 0:1]), "carry_b")
            v.wait_ge(s_mid_pe, -(-BLOCKS // 4) + 3)
            link(v.tensor_copy(crow[:, 0:2, 0:P], ps[4][0:1, 0:2 * P].rearrange("p (k i) -> p k i", k=2)))
            link(v.tensor_tensor_scan(crow[:, 2, 0:P][:, ::-1], crow[:, 1, 0:P][:, ::-1], crow[:, 0, 0:P][:, ::-1],
                                      LOWEST, ALU.add, ALU.max))
            link(v.memset(crow[:, 2, P:P + 1], LOWEST), "crow_b")
            v.wait_ge(s_mid_pe, -(-BLOCKS // 4) + 4)
            link(v.tensor_copy(carry[:, 3:4], ps[5][:, 0:1]))
            link(v.tensor_tensor_scan(MT[:, ::-1], pen[:, ::-1], FT[:, ::-1], carry[:, 3:4], ALU.add, ALU.max))
            link(v.tensor_tensor(FT, ST, MT, ALU.subtract), "diff")
            for b in range(BLOCKS):
                v.wait_ge(s_back_pe, b + 1)
                v.tensor_copy(SWt[:, b], ps[b % 4][:, 0:P].rearrange("p (h g) -> p h g", h=HEADS)).then_inc(s_back_cp, 1)
            v.wait_ge(s_back_cp, BLOCKS)

            def spread(s, e, j):
                v.tensor_copy(SW[:, bass.ds(s + EDGE_TILES, 1), :], SW[:, bass.ds(e, 1), :]).then_inc(s_fold, 1)

            with v.Fori(0, EXTRA // RING) as r:
                e = edge_tiles(r * RING, RING)
                for k in range(RING):
                    spread(r * RING + k, e[k], k)
            v.wait_ge(s_fold, 2 * EXTRA)
            link(v.memset(SUMS[:], 0.0), "weights0")

            def add(s, bank, w, width, g):
                v.wait_ge(g["summed"], s + 1)
                at_least(v, g["added"], s)
                v.tensor_tensor(SUMS[:, bass.ds(w, 1), 0:width], SUMS[:, bass.ds(w, 1), 0:width],
                                ps[bank][:, 0:width].rearrange("p (a f) -> p a f", a=1), ALU.add).then_inc(g["added"], 1)

            def sum_pass(g, width, weighted):
                for s in range(LAG):
                    build(s, s, g["summed"], 0, g["onehot"], weighted)
                rounds = STEPS // RING

                def step(s, k, w):
                    if not (isinstance(s, int) and s + LAG >= STEPS):
                        build(s + LAG, (k + LAG) % RING, g["summed"], s + LAG - RING + 1, g["onehot"], weighted)
                    add(s, k, w, width, g)

                w = windows(0, RING)
                for s in range(RING):
                    step(s, s, w[s])
                with v.Fori(1, rounds) as r:
                    w = windows(r * RING, RING)
                    for k in range(RING):
                        step(r * RING + k, k, w[k])
                w = windows(rounds * RING, STEPS - rounds * RING)
                for s in range(rounds * RING, STEPS):
                    step(s, s % RING, w[s % RING])
                v.wait_ge(g["added"], STEPS)

            sum_pass(a0, ACCW, False)
            SUMh = SUMS[:, :, 0:F]
            den = SUMS[:, :, F:F + HEADS]
            deg = SUMS[:, :, F + HEADS]
            link(v.scalar_tensor_tensor(rden[:], den, 0.0, den, ALU.is_equal, ALU.add))
            link(v.reciprocal(rden[:], rden[:]))
            link(v.scalar_tensor_tensor(dtmp[:, 0, :], deg, 0.0, deg, ALU.is_equal, ALU.add), "deg")

            def p0_in(s, k):
                at_least(v, p0["turned"], s - 1)
                v.tensor_tensor(hs[:, k, :].rearrange("p (h d) -> p h d", h=HEADS),
                                SUMS[:, bass.ds(s, 1), 0:F].rearrange("p a (h d) -> p (a h) d", h=HEADS),
                                rden[:, bass.ds(s, 1), :].rearrange("p a h -> p (a h)").unsqueeze(2).to_broadcast([P, HEADS, HDIM]),
                                ALU.mult).then_inc(p0["inn"], 1)

            def p0_tile(s, k, r):
                if not (isinstance(s, int) and s + 1 >= NODE_TILES):
                    p0_in(s + 1, (k + 1) % 2)
                v.wait_ge(p0["prod"], s + 1)
                v.tensor_tensor(X[:, bass.ds(s, 1), :], X[:, bass.ds(s, 1), :],
                                ps[2 + k][:, 0:F].rearrange("p (a f) -> p a f", a=1), ALU.add).then_inc(p0["x"], 1)
                v.wait_ge(p0["x"], s + 1)
                v.bn_stats(stats[:, bass.ds(s, 1), :], X[:, bass.ds(s, 1), :]).then_inc(p0["stats"], 1)

            v.wait_ge(d0["xadd"], NODE_TILES)
            p0_in(0, 0)
            rolled(v, 0, NODE_TILES, 2, p0_tile)
            norm_stats(p0["stats"])
            norm_scale(1)
            v.wait_ge(s_dq, 1)
            link(v.reciprocal(dtmp[:, 1, :], dtmp[:, 0, :]))
            link(v.scalar_tensor_tensor(dinv[:], deg, 0.0, dtmp[:, 1, :], ALU.is_gt, ALU.mult))

            v.wait_ge(s_h1, NODE_TILES)
            link(v.tensor_copy(Tst[:, :, F], dinv[:]))
            link(v.tensor_tensor(Tst[:, :, 0:F], H[:], dinv[:].unsqueeze(2).to_broadcast([P, NODE_TILES, F]),
                                 ALU.mult), "t1")
            link(v.memset(SUMS[:], 0.0))
            sum_pass(g1, F + 1, False)

            def p1_in(s, k):
                at_least(v, p1["turned"], s - 1)
                v.tensor_tensor(hs[:, k, :].rearrange("p (a f) -> p a f", a=1), SUMS[:, bass.ds(s, 1), 0:F],
                                H[:, bass.ds(s, 1), :], ALU.mult).then_inc(p1["inn"], 1)

            def p1_tile(s, k, r):
                if not (isinstance(s, int) and s + 1 >= NODE_TILES):
                    p1_in(s + 1, (k + 1) % 2)
                v.wait_ge(p1["prod"], s + 1)
                v.wait_ge(p1["hb"], s + 1)
                v.scalar_tensor_tensor(y[:, k, :], hb[:, k, :], SUMS[:, bass.ds(s, 1), F:F + 1].rearrange("p a b -> p (a b)"),
                                       ps[2 + k][:, 0:F], ALU.mult, ALU.add).then_inc(p1["y"], 1)
                v.wait_ge(p1["y"], s + 1)
                v.scalar_tensor_tensor(y[:, k, :], y[:, k, :], SLOPE, y[:, k, :], ALU.mult, ALU.max).then_inc(p1["z"], 1)
                v.wait_ge(p1["z"], s + 1)
                v.scalar_tensor_tensor(X[:, bass.ds(s, 1), :], y[:, k, :].rearrange("p (a f) -> p a f", a=1),
                                       dinv[:, bass.ds(s, 1)], X[:, bass.ds(s, 1), :], ALU.mult, ALU.add).then_inc(p1["x"], 1)
                v.wait_ge(p1["x"], s + 1)
                v.bn_stats(stats[:, bass.ds(s, 1), :], X[:, bass.ds(s, 1), :]).then_inc(p1["stats"], 1)

            p1_in(0, 0)
            rolled(v, 0, NODE_TILES, 2, p1_tile)
            norm_stats(p1["stats"])
            norm_scale(2)

            half = RELS // 2 * F

            def store_free(d, s, k, r):
                if not (isinstance(r, int) and r == 0):
                    v.wait_ge(d["stored"][k], 16 * r)

            def d2_tile(s, k, r):
                hT_copy(d2, s, k)
                v.wait_ge(d2["gexp"], s + 1)
                v.tensor_scalar(gate[:, k, 1, :], gate[:, k, 0, :], 1.0, None, ALU.add).then_inc(d2["gone"], 1)
                v.wait_ge(d2["gone"], s + 1)
                at_least(v, d2["act"], s - 1)
                v.reciprocal(gate[:, k, 0, :], gate[:, k, 1, :]).then_inc(d2["gsig"], 1)
                v.wait_ge(d2["gsig"], s + 1)
                v.wait_ge(d2["prod"], s + 1)
                store_free(d2, s, k, r)
                v.tensor_tensor(stage[:, k, 0:half].rearrange("p (q f) -> p q f", f=F),
                                ps[4 + 2 * k][:].rearrange("p (q f) -> p q f", f=F),
                                gate[:, k, 0, 0:RELS // 2].unsqueeze(2).to_broadcast([P, RELS // 2, F]),
                                ALU.mult).then_inc(d2["dve"], 1)

            rolled(v, 0, NODE_TILES, 2, d2_tile)
            link(v.memset(SUMS[:], 0.0))
            sum_pass(gr2, F, True)
            link(v.scalar_tensor_tensor(X[:], SUMh, 0.0, X[:], ALU.max, ALU.add))
            rolled(v, 0, NODE_TILES, 4, lambda s, k, r: v.bn_stats(
                stats[:, bass.ds(s, 1), :], X[:, bass.ds(s, 1), :]).then_inc(p2["stats"], 1))
            norm_stats(p2["stats"])
            norm_scale(3)

            def d3_tile(s, k, r):
                hT_copy(d3, s, k)
                v.wait_ge(d3["prod"], s + 1)
                store_free(d3, s, k, r)
                v.tensor_copy(stage[:, k, 0:half], ps[4 + 2 * k][:]).then_inc(d3["dve"], 1)

            rolled(v, 0, NODE_TILES, 2, d3_tile)
            link(v.memset(SUMS[:], 0.0))
            sum_pass(gr3, F, False)
            v.wait_ge(d3["xadd"], NODE_TILES)
            link(v.tensor_tensor(X[:], SUMh, X[:], ALU.add), "final")

        @block.gpsimd
        def _(g):
            g.iota(iota_row[:], [[1, P]], base=0, channel_multiplier=0, allow_small_or_imprecise_dtypes=True)
            g.iota(iota_col[:], [[0, 1]], base=0, channel_multiplier=1, allow_small_or_imprecise_dtypes=True)
            g.iota(next_row[:], [[1, EXTRA]], base=1, channel_multiplier=0, allow_small_or_imprecise_dtypes=True)
            g.iota(next_col[:], [[0, 1]], base=1, channel_multiplier=1, allow_small_or_imprecise_dtypes=True)
            g.memset(X[:, NODE_TILES - 1, :], 0.0)
            g.memset(RI[:, :, 0, :], NO_NODE)
            g.memset(RI[:, :, 1:3, :], 0)
            g.memset(R[:, :, 3, :], 0.0)
            g.memset(one[:], 1.0)
            g.memset(minus1[:, 0:1], -1)
            g.memset(minus1[:, 1:2], NO_NODE)
            g.memset(minus1[:, 2:3], 0)
            g.memset(SW[:], 1.0)
            g.iota(tile[:], [[1, EXTRA]], base=1, channel_multiplier=0).then_inc(s_const, 1)

            g.wait_ge(dve_step, mark["tiles"])
            g.wait_ge(s_scratch, 16 * 6)
            g.indirect_dma_start(xrows[0:EXTRA, :], None, rows_d[:, :],
                                 bass.IndirectOffsetOnAxis(ap=few[0:EXTRA, 0:1], axis=0)).then_inc(s_extra, 16)

            def xadd(d, s, k):
                g.wait_ge(d["h"], s + 1)
                g.tensor_tensor(X[:, bass.ds(s, 1), :], X[:, bass.ds(s, 1), :],
                                hs[:, k, :].rearrange("p (a f) -> p a f", a=1), ALU.add).then_inc(d["xadd"], 1)

            rolled(g, 0, NODE_TILES, 2, lambda s, k, r: xadd(d0, s, k))

            def gather(q, table, width, freed, written):
                def body(s, k, r):
                    for name, free in freed:
                        if name == "step":
                            at_least(g, free, s - RING + 1)
                        elif not (isinstance(r, int) and r == 0):
                            g.wait_ge(free[k], 16 * r)
                    for d, n in written:
                        g.wait_ge(d, n)
                    g.wait_ge(q["idx"], s + 1)
                    g.sem_inc(q["issued"], 1)
                    g.indirect_dma_start(ring[:, k, 0:width], None, table,
                                         bass.IndirectOffsetOnAxis(ap=idx[:, k:k + 1], axis=0)).then_inc(q["rows"][k], 16)
                rolled(g, 0, STEPS, RING, body)

            table_done = [(d0["stored"][0], 16 * (NODE_TILES // 2 + 1)), (d0["stored"][1], 16 * (NODE_TILES // 2))]
            gather(q0, qv_d[:, :], 2 * F, [("step", q0["prod"]), ("slot", q0["saved"])], table_done)

            g.wait_ge(dve_step, mark["weights0"])

            def weigh(s, k, r):
                g.wait_ge(a0["loaded"][k // RING], 16 * (r + 1))
                at_least(g, a0["summed"], s - RING + 1)
                g.tensor_tensor(vw[:, k % RING, 0:F].rearrange("p (h d) -> p h d", h=HEADS),
                                vin[:, k // RING, k % RING, :].rearrange("p (h d) -> p h d", h=HEADS),
                                SW[:, bass.ds(s, 1), 0:HEADS].rearrange("p a h -> p (a h)").unsqueeze(2).to_broadcast([P, HEADS, HDIM]),
                                ALU.mult).then_inc(a0["vw"], 1)

            rolled(g, 0, STEPS, UNROLL2, weigh)

            gather(g1, t1_d[:, :], F + 1, [("step", g1["summed"])], [(s_t1d, 16)])

            def add_bias(s, k, r):
                at_least(g, p1["y"], s - 1)
                g.tensor_tensor(hb[:, k, :].rearrange("p (a f) -> p a f", a=1), H[:, bass.ds(s, 1), :],
                                bias[:].rearrange("p (a f) -> p a f", a=1), ALU.add).then_inc(p1["hb"], 1)

            rolled(g, 0, NODE_TILES, 2, add_bias)
            table_done = [(d2["stored"][0], 16 * (NODE_TILES // 2 + 1)), (d2["stored"][1], 16 * (NODE_TILES // 2))]
            gather(gr2, t2_d[:, :], F, [("step", gr2["summed"])], table_done)
            rolled(g, 0, NODE_TILES, 2, lambda s, k, r: xadd(d3, s, k))
            table_done = [(d3["stored"][0], 16 * (NODE_TILES // 2 + 1)), (d3["stored"][1], 16 * (NODE_TILES // 2))]
            gather(gr3, t3_d[:, :], F, [("step", gr3["summed"])], table_done)

        @block.scalar
        def _(a):
            def root(n):
                a.wait_ge(dve_step, mark[f"var{n}"])
                a.activation(ln[:, 3, :], ln[:, 3, :], ACT.Sqrt).then_inc(s_lnsq, 1)

            def normed(d, n, s, k, tgt=None):
                at_least(a, d["turned"], s - 1)
                if "xadd" in d:
                    at_least(a, d["xadd"], s - 1)
                a.activation(hs[:, k, :].rearrange("p (a f) -> p a f", a=1), X[:, bass.ds(s, 1), :], ACT.Relu,
                             bias=shift[:, bass.ds(s, 1)], scale=rstd[:, bass.ds(s, 1)]).then_inc(d["h"], 1)

            root(0)
            a.wait_ge(dve_step, mark["ln0"])

            def d0_tile(s, k, r):
                if not (isinstance(s, int) and s + 1 >= NODE_TILES):
                    normed(d0, 0, s + 1, (k + 1) % 2)
                a.wait_ge(d0["prod"], s + 1)
                if not (isinstance(r, int) and r == 0):
                    a.wait_ge(d0["stored"][k], 16 * r)
                a.activation(stage[:, k, 0:2 * F], ps[2 + k][:, 0:2 * F], ACT.Copy).then_inc(d0["qv"], 1)

            normed(d0, 0, 0, 0)
            rolled(a, 0, NODE_TILES, 2, d0_tile)

            def index(q, kind, s, k, r):
                if not (isinstance(r, int) and r == 0):
                    a.wait_ge(q["rows"][k], 16 * r)
                a.activation(idx[:, k:k + 1], col[:, kind, bass.ds(s, 1)], ACT.Copy).then_inc(q["idx"], 1)

            a.wait_ge(dve_step, mark["cols"])

            for s in range(RING):
                index(q0, 1, s, s, 0)

            def q0_step(s, k, r):
                a.wait_ge(q0["turned"], s + 1)
                at_least(a, q0["kexp"], s - RING + 1)
                a.activation(onehotT[:, k, :], ps[k][:, 0:P], ACT.Copy).then_inc(q0["copied"], 1)
                if not (isinstance(s, int) and s + RING >= STEPS):
                    index(q0, 1, s + RING, k, r + 1)

            last = STEPS // RING - 1
            for s in range(RING):
                q0_step(s, s, 0)
            with a.Fori(1, last) as r:
                for k in range(RING):
                    q0_step(r * RING + k, k, r)
            for s in range(last * RING, STEPS):
                q0_step(s, s % RING, s // RING)

            a.wait_ge(dve_step, mark["diff"])
            a.activation(ST, FT, ACT.Exp).then_inc(act_step, 1)

            a.wait_ge(dve_step, mark["weights0"])

            def wcol(s, k, r):
                at_least(a, a0["summed"], s - RING + 1)
                a.activation(vw[:, k, F:ACCW].rearrange("p (a f) -> p a f", a=1), SW[:, bass.ds(s, 1), :],
                             ACT.Copy).then_inc(a0["wcol"], 1)

            rolled(a, 0, STEPS, RING, wcol)
            a.wait_ge(dve_step, mark["deg"])
            a.activation(dtmp[:, 0, :], dtmp[:, 0, :], ACT.Sqrt).then_inc(s_dq, 1)

            def turned_copy(p, s, k, r):
                a.wait_ge(p["turned"], s + 1)
                at_least(a, p["prod"], s - 1)
                a.activation(hT[:, k, :], ps[k][:, 0:F], ACT.Copy).then_inc(p["T"], 1)

            rolled(a, 0, NODE_TILES, 2, lambda s, k, r: turned_copy(p0, s, k, r))
            root(1)
            a.wait_ge(dve_step, mark["ln1"])
            rolled(a, 0, NODE_TILES, 4, lambda s, k, r: a.activation(
                H[:, bass.ds(s, 1), :], X[:, bass.ds(s, 1), :], ACT.Relu,
                bias=shift[:, bass.ds(s, 1)], scale=rstd[:, bass.ds(s, 1)]).then_inc(s_h1, 1))

            rolled(a, 0, STEPS, RING, lambda s, k, r: index(g1, 1, s, k, r))
            rolled(a, 0, NODE_TILES, 2, lambda s, k, r: turned_copy(p1, s, k, r))
            root(2)
            a.wait_ge(dve_step, mark["ln2"])

            half = RELS // 2

            def d2_tile(s, k, r):
                if not (isinstance(s, int) and s + 1 >= NODE_TILES):
                    normed(d2, 2, s + 1, (k + 1) % 2)
                a.wait_ge(d2["gate"], s + 1)
                at_least(a, d2["dve"], s - 1)
                at_least(a, d2["act"], s - 1)
                a.activation(gate[:, k, 0, :], ps[2 + k][:, 0:RELS], ACT.Exp, scale=-1.0).then_inc(d2["gexp"], 1)
                a.wait_ge(d2["gsig"], s + 1)
                a.wait_ge(d2["prod"], s + 1)
                if not (isinstance(r, int) and r == 0):
                    a.wait_ge(d2["stored"][k], 16 * r)
                for q in range(half):
                    ins = a.activation(stage[:, k, (half + q) * F:(half + q + 1) * F],
                                       ps[5 + 2 * k][:, q * F:(q + 1) * F], ACT.Copy,
                                       scale=gate[:, k, 0, half + q:half + q + 1])
                ins.then_inc(d2["act"], 1)

            normed(d2, 2, 0, 0)
            rolled(a, 0, NODE_TILES, 2, d2_tile)
            rolled(a, 0, STEPS, RING, lambda s, k, r: index(gr2, 2, s, k, r))
            root(3)
            a.wait_ge(dve_step, mark["ln3"])

            def d3_tile(s, k, r):
                if not (isinstance(s, int) and s + 1 >= NODE_TILES):
                    normed(d3, 3, s + 1, (k + 1) % 2)
                a.wait_ge(d3["prod"], s + 1)
                if not (isinstance(r, int) and r == 0):
                    a.wait_ge(d3["stored"][k], 16 * r)
                a.activation(stage[:, k, half * F:RELS * F], ps[5 + 2 * k][:], ACT.Copy).then_inc(d3["act"], 1)

            normed(d3, 3, 0, 0)
            rolled(a, 0, NODE_TILES, 2, d3_tile)
            rolled(a, 0, STEPS, RING, lambda s, k, r: index(gr3, 2, s, k, r))

        @block.tensor
        def _(t):
            win_regs = [t.alloc_register(f"pwin{k}") for k in range(RING)]

            def windows(s, n):
                t.reg_load(win_regs[0:n], win[0:1, bass.ds(s, n)])
                return [t.snap(r, min_val=0, max_val=NODE_TILES - 1) for r in win_regs[0:n]]

            t.wait_ge(dve_step, mark["rows"])
            t.wait_ge(s_edges, 12 * 16)
            for c in range(CHUNKS):
                n = P if c < CHUNKS - 1 else CTAIL
                for kind in range(4):
                    ins = t.transpose(ps[c][:, kind * P:kind * P + n], R[0:n, c, kind, :], ident[0:n, 0:n])
                ins.then_inc(pe_prep, 1)
            t.wait_ge(s_extra, 16)
            for kind in range(4):
                ins = t.transpose(ps[CHUNKS][:, kind * P:kind * P + EXTRA], xrows[0:EXTRA, kind * P:(kind + 1) * P],
                                  ident[0:EXTRA, 0:EXTRA])
            ins.then_inc(pe_prep, 1)
            t.wait_ge(s_w, 16 * 9)
            t.wait_ge(dve_step, mark["wsum"])
            for j in range(4):
                t.transpose(ps[0][:, j * F:(j + 1) * F], wraw[:, j, :], ident[:])
            t.transpose(ps[1][:, 0:F], hs[:, 0, :], ident[:]).then_inc(pe_prep, 1)

            def turn(d_in, d, s, k):
                t.wait_ge(d_in, s + 1)
                t.transpose(ps[k][:, 0:F], hs[:, k, :], ident[:]).then_inc(d["turned"], 1)

            t.wait_ge(dve_step, mark["weights"])

            def d0_turn(s, k):
                at_least(t, d0["hT"], s - 1)
                turn(d0["h"], d0, s, k)

            def d0_tile(s, k, r):
                if not (isinstance(s, int) and s + 1 >= NODE_TILES):
                    d0_turn(s + 1, (k + 1) % 2)
                t.wait_ge(d0["hT"], s + 1)
                at_least(t, d0["qv"], s - 1)
                at_least(t, d0["k"], s - 1)
                t.matmul(ps[2 + k][:, 0:2 * F], hT[:, k, :], wqkvT[:, 0:2 * F], start=True, stop=True)
                t.matmul(ps[4 + k][:, 0:F], hT[:, k, :], wqkvT[:, 2 * F:3 * F], start=True, stop=True).then_inc(d0["prod"], 1)

            d0_turn(0, 0)
            rolled(t, 0, NODE_TILES, 2, d0_tile)

            t.wait_ge(d0["k"], NODE_TILES)
            t.wait_ge(d0["qv"], NODE_TILES)
            t.wait_ge(s_scratch, 16 * 8)

            def q0_turn(s, k):
                t.wait_ge(q0["onehot"], s + 1)
                at_least(t, q0["copied"], s - RING + 1)
                t.transpose(ps[k][:, 0:P], onehot[:, k, :], ident[:]).then_inc(q0["turned"], 1)

            def q0_step(s, k, r, w):
                if not (isinstance(s, int) and s + 1 >= STEPS):
                    q0_turn(s + 1, (k + 1) % RING)
                t.wait_ge(q0["copied"], s + 1)
                at_least(t, q0["prod"], s - RING + 1)
                t.matmul(ps[4 + k][:, 0:F], onehotT[:, k, :], K[:, bass.ds(w, 1), :].rearrange("p a f -> p (a f)"),
                         start=True, stop=True).then_inc(q0["kexp"], 1)

            q0_turn(0, 0)
            rounds = STEPS // RING
            w = windows(0, RING)
            for s in range(RING):
                q0_step(s, s, 0, w[s])
            with t.Fori(1, rounds) as r:
                w = windows(r * RING, RING)
                for k in range(RING):
                    q0_step(r * RING + k, k, r, w[k])
            w = windows(rounds * RING, STEPS - rounds * RING)
            for s in range(rounds * RING, STEPS):
                q0_step(s, s % RING, rounds, w[s % RING])

            t.wait_ge(dve_step, mark["blocks"])
            n4 = -(-BLOCKS // 4)
            for b in range(0, BLOCKS, 4):
                at_least(t, s_mid_cp, b // 4 - 1)
                for j in range(min(4, BLOCKS - b)):
                    ins = t.transpose(ps[(b // 4) % 2][:, j * P:(j + 1) * P], FT[:, (b + j) * P:(b + j + 1) * P], ident[:])
                ins.then_inc(s_mid_pe, 1)
            for name, bank in (("f", 2), ("b", 4)):
                t.wait_ge(dve_step, mark["carry_" + name])
                t.transpose(ps[bank][0:1, 0:P], carry[:, 0:1], ident[:])
                t.transpose(ps[bank][0:1, P:2 * P], carry[:, 1:2], ident[:]).then_inc(s_mid_pe, 1)
                t.wait_ge(dve_step, mark["crow_" + name])
                o = 0 if name == "f" else 1
                t.matmul(ps[bank + 1][:, 0:1], crow[0:1, 2, o:o + P], one[0:1, 0:1], start=True, stop=True).then_inc(s_mid_pe, 1)
            t.wait_ge(act_step, 1)
            for b in range(BLOCKS):
                at_least(t, s_back_cp, b - 3)
                t.transpose(ps[b % 4][:, 0:P], ST[:, b * P:(b + 1) * P], ident[:]).then_inc(s_back_pe, 1)

            def a0_step(s, k, r):
                t.wait_ge(a0["onehot"], s + 1)
                t.wait_ge(a0["vw"], s + 1)
                t.wait_ge(a0["wcol"], s + 1)
                at_least(t, a0["added"], s - RING + 1)
                t.matmul(ps[k][:, 0:ACCW], onehot[:, k, :], vw[:, k, :], start=True, stop=True).then_inc(a0["summed"], 1)

            t.wait_ge(s_back_cp, BLOCKS)
            rolled(t, 0, STEPS, RING, a0_step)

            def node_product(p, weight, free):
                def turn_in(s, k):
                    at_least(t, p["T"], s - 1)
                    turn(p["inn"], p, s, k)

                def body(s, k, r):
                    if not (isinstance(s, int) and s + 1 >= NODE_TILES):
                        turn_in(s + 1, (k + 1) % 2)
                    t.wait_ge(p["T"], s + 1)
                    at_least(t, free, s - 1)
                    t.matmul(ps[2 + k][:, 0:F], hT[:, k, :], weight, start=True, stop=True).then_inc(p["prod"], 1)

                turn_in(0, 0)
                rolled(t, 0, NODE_TILES, 2, body)

            t.wait_ge(a0["added"], STEPS)
            node_product(p0, wsT[:], p0["x"])

            def sum_step(g):
                def body(s, k, r, width):
                    t.wait_ge(g["onehot"], s + 1)
                    t.wait_ge(g["rows"][k], 16 * (r + 1))
                    at_least(t, g["added"], s - RING + 1)
                    t.matmul(ps[k][:, 0:width], onehot[:, k, :], ring[:, k, 0:width], start=True, stop=True).then_inc(g["summed"], 1)
                return body

            t.wait_ge(p0["x"], NODE_TILES)
            body1 = sum_step(g1)
            rolled(t, 0, STEPS, RING, lambda s, k, r: body1(s, k, r, F + 1))
            t.wait_ge(g1["added"], STEPS)
            node_product(p1, w1T[:], p1["y"])

            def relations(d, w, gated):
                def turn_in(s, k):
                    at_least(t, d["hT"], s - 1)
                    turn(d["h"], d, s, k)

                def body(s, k, r):
                    if not (isinstance(s, int) and s + 1 >= NODE_TILES):
                        turn_in(s + 1, (k + 1) % 2)
                    t.wait_ge(d["hT"], s + 1)
                    if gated:
                        at_least(t, d["gexp"], s - 1)
                        t.matmul(ps[2 + k][:, 0:RELS], hT[:, k, :], g2[:], start=True, stop=True).then_inc(d["gate"], 1)
                    at_least(t, d["dve"], s - 1)
                    at_least(t, d["act"], s - 1)
                    half = RELS // 2
                    t.matmul(ps[4 + 2 * k][:], hT[:, k, :], w[:, 0:half, :].rearrange("p q f -> p (q f)"), start=True, stop=True)
                    t.matmul(ps[5 + 2 * k][:], hT[:, k, :], w[:, half:RELS, :].rearrange("p q f -> p (q f)"),
                             start=True, stop=True).then_inc(d["prod"], 1)

                turn_in(0, 0)
                rolled(t, 0, NODE_TILES, 2, body)

            t.wait_ge(p1["y"], NODE_TILES)
            relations(d2, w2, True)
            body2 = sum_step(gr2)
            t.wait_ge(d2["dve"], NODE_TILES)
            t.wait_ge(d2["act"], NODE_TILES)
            rolled(t, 0, STEPS, RING, lambda s, k, r: body2(s, k, r, F))
            t.wait_ge(gr2["added"], STEPS)
            relations(d3, w3, False)
            body3 = sum_step(gr3)
            t.wait_ge(d3["dve"], NODE_TILES)
            t.wait_ge(d3["act"], NODE_TILES)
            rolled(t, 0, STEPS, RING, lambda s, k, r: body3(s, k, r, F))

        @block.sync
        def _(sp):
            full = (NODE_TILES - 1) * P
            sp.wait_ge(s_const, 1)
            sp.dma_start(X[:, 0:NODE_TILES - 1, :], x[0:full, :].rearrange("(t p) f -> p t f", p=P)).then_inc(s_x, 16)
            sp.dma_start(X[0:NTAIL, NODE_TILES - 1, :], x[full:N, :]).then_inc(s_x, 16)
            c6 = (CHUNKS - 1) * P * P
            tail = (EDGE_TILES - 1) * P
            for kind, a in ((0, dst), (1, src), (2, rel), (3, weight1)):
                t_ = R[:, :, 3, :] if kind == 3 else RI[:, :, kind, :]
                sp.dma_start(t_[:, 0:CHUNKS - 1, :], a[0:c6].rearrange("(c p i) -> p c i", p=P, i=P)).then_inc(s_edges, 16)
                sp.dma_start(t_[0:CTAIL - 1, CHUNKS - 1, :], a[c6:tail].rearrange("(p i) -> p i", i=P)).then_inc(s_edges, 16)
                sp.dma_start(t_[CTAIL - 1:CTAIL, CHUNKS - 1, 0:ETAIL], a[tail:E].rearrange("(a i) -> a i", a=1)).then_inc(s_edges, 16)
            for j, w in enumerate((Wq, Wk, Wv, W1)):
                sp.dma_start(wraw[:, j, :], w).then_inc(s_w, 16)
            sp.dma_start(wsraw[:], Wscale.rearrange("(h i) c -> i h c", h=HEADS)).then_inc(s_w, 16)
            sp.dma_start(w2[:], W2.rearrange("r d f -> d r f")).then_inc(s_w, 16)
            sp.dma_start(w3[:], W3.rearrange("r d f -> d r f")).then_inc(s_w, 16)
            sp.dma_start(g2[:], gate2.rearrange("r d o -> d (r o)"), allow_slow_non_contiguous=True).then_inc(s_w, 16)
            sp.dma_start(bias[:], bass.AP(b1.tensor, 0, [[0, P], [1, F]])).then_inc(s_w, 16)

            sp.wait_ge(dve_step, mark["rows"])
            nfull = (CHUNKS - 1) * P
            sp.dma_start(win_d[1:1 + nfull].rearrange("(c p) -> p c", p=P), ends[:, 0:CHUNKS - 1], allow_slow_non_contiguous=True).then_inc(s_scratch, 16)
            sp.dma_start(win_d[1 + nfull:EDGE_TILES].rearrange("(p a) -> p a", a=1),
                         ends[0:CTAIL - 1, CHUNKS - 1:CHUNKS]).then_inc(s_scratch, 16)
            sp.dma_start(win_d[0:1].rearrange("(a b) -> a b", a=1), minus1[:, 2:3]).then_inc(s_scratch, 16)
            sp.dma_start(win_d[EDGE_TILES:STEPS].rearrange("(a b) -> a b", a=1), tile[:]).then_inc(s_scratch, 16)
            sp.dma_start(rows_d[0:nfull, :].rearrange("(c p) f -> p c f", p=P),
                         R[:, 0:CHUNKS - 1].rearrange("p c k i -> p c (k i)")).then_inc(s_scratch, 16)
            sp.dma_start(rows_d[nfull:EDGE_TILES, :], R[0:CTAIL, CHUNKS - 1].rearrange("p k i -> p (k i)")).then_inc(s_scratch, 16)
            sp.dma_start(dst_d[1:1 + nfull * P].rearrange("(c p i) -> p c i", p=P, i=P), RI[:, 0:CHUNKS - 1, 0, :]).then_inc(s_dpad, 16)
            rest = GROUPS * BLOCKS - nfull
            sp.dma_start(dst_d[1 + nfull * P:1 + GROUPS * ROW].rearrange("(p i) -> p i", i=P), RI[0:rest, CHUNKS - 1, 0, :]).then_inc(s_dpad, 16)
            sp.dma_start(dst_d[0:1].rearrange("(a b) -> a b", a=1), minus1[:, 0:1]).then_inc(s_dpad, 16)
            sp.dma_start(dst_d[GROUPS * ROW + 1:GROUPS * ROW + 2].rearrange("(a b) -> a b", a=1), minus1[:, 1:2]).then_inc(s_dpad, 16)
            sp.wait_ge(s_scratch, 16 * 6)
            sp.dma_start(winb_i, bass.AP(win_d.tensor, 0, [[0, P], [1, EDGE_TILES]])).then_inc(s_scratch, 16)
            sp.dma_start(win[:], win_d.rearrange("(a b) -> a b", a=1)).then_inc(s_scratch, 16)
            sp.wait_ge(dve_step, mark["tiles"])
            sp.wait_ge(s_scratch, 16 * 8)
            sp.dma_start(tile_d.rearrange("(p a) -> p a", a=1), few[0:EXTRA, 0:1]).then_inc(s_scratch, 16)
            sp.wait_ge(s_scratch, 16 * 9)
            sp.dma_start(tile[:], tile_d.rearrange("(a b) -> a b", a=1)).then_inc(s_scratch, 16)
            sp.wait_ge(s_dpad, 64)
            sp.wait_ge(dve_step, mark["cols"])
            for h in range(HEADS):
                sp.dma_start(drow[h * GROUPS:(h + 1) * GROUPS, :],
                             bass.AP(dst_d.tensor, 0, [[ROW, GROUPS], [1, ROW + 2]])).then_inc(s_drow, 16)

            def store(d, table, width, waits):
                def body(s, k, r):
                    for w in waits:
                        sp.wait_ge(w, s + 1)
                    sp.dma_start(table[bass.ds(s * P, P), :], stage[:, k, 0:width]).then_inc(d["stored"][k], 16)
                rolled(sp, 0, NODE_TILES, 2, body)

            store(d0, qv_d, 2 * F, [d0["qv"]])

            def save(s, k, r):
                sp.wait_ge(q0["rows"][k], 16 * (r + 1))
                sp.dma_start(v_d[:, bass.ds(s, 1), :], ring[:, k, F:2 * F].rearrange("p (a f) -> p a f", a=1)).then_inc(q0["saved"][k], 16)

            rolled(sp, 0, STEPS, RING, save)
            for k in range(RING):
                sp.wait_ge(q0["saved"][k], 16 * (STEPS // RING + (k < STEPS % RING)))

            def load(b, j, r):
                n = RING if not isinstance(b, int) else min(RING, STEPS - b * RING)
                at_least(sp, a0["vw"], (b - VRING + 1) * RING)
                sp.dma_start(vin[:, j, 0:n, :], v_d[:, bass.ds(b * RING, n), :]).then_inc(a0["loaded"][j], 16)

            rolled(sp, 0, -(-STEPS // RING), VRING, load)

            sp.wait_ge(dve_step, mark["t1"])
            sp.dma_start(t1_d.rearrange("(t p) f -> p t f", p=P), Tst).then_inc(s_t1d, 16)
            store(d2, t2_d.rearrange("(n r) f -> n (r f)", r=RELS), RELS * F, [d2["dve"], d2["act"]])
            store(d3, t3_d.rearrange("(n r) f -> n (r f)", r=RELS), RELS * F, [d3["dve"], d3["act"]])
            sp.wait_ge(dve_step, mark["final"])
            sp.dma_start(out[0:full, :].rearrange("(t p) f -> p t f", p=P), X[:, 0:NODE_TILES - 1, :]).then_inc(s_out, 16)
            sp.dma_start(out[full:N, :], X[0:NTAIL, NODE_TILES - 1, :]).then_inc(s_out, 16)
            sp.wait_ge(s_out, 32)


_INS = ["x", "src", "dst", "edge_type_8", "edge_weight1", "L0_gnn_Wq", "L0_gnn_Wk", "L0_gnn_Wv", "L0_gnn_Wscale",
        "L1_gnn_W1_w", "L1_gnn_W1_b", "L2_gnn_weight", "L2_gnn_gate_weight", "L3_gnn_W"]


def kernel(**inputs):
    import numpy as np
    import concourse.bacc as bacc
    from concourse.bass_utils import run_bass_kernel_spmd

    nc = bacc.Bacc("TRN2", target_bir_lowering=False, num_devices=1)
    arrays, args = {}, []
    for name in _INS:
        a = np.ascontiguousarray(inputs[name])
        if name == "edge_weight1":
            a = a.reshape(-1)
        arrays["in_" + name] = a
        args.append(nc.dram_tensor("in_" + name, a.shape, mybir.dt.from_np(a.dtype), kind="ExternalInput").ap())
    out = nc.dram_tensor("out", (N, F), F32, kind="ExternalOutput").ap()
    graph_layers(nc, *args, out)
    return run_bass_kernel_spmd(nc, [arrays], core_ids=[0]).results[0]["out"]
```

```python
from contextlib import ExitStack

import concourse.bass as bass
from concourse import mybir

P = 128
N, E, F = 6250, 100000, 128
HEADS, HDIM = 4, 32
RELS = 8
EPS = 1e-5
SLOPE = 0.01

NODE_TILES = -(-N // P)
NPAD = NODE_TILES * P
NTAIL = N - (NODE_TILES - 1) * P
EDGE_TILES = -(-E // P)
ETAIL = E - (EDGE_TILES - 1) * P
EXTRA = NODE_TILES - 1
STEPS = EDGE_TILES + EXTRA
CHUNKS = -(-EDGE_TILES // P)
CTAIL = EDGE_TILES - (CHUNKS - 1) * P

GROUPS = P // HEADS
BLOCKS = -(-EDGE_TILES // GROUPS)
ROW = BLOCKS * P

RING = 8
BANKS = 4
VB, VSLOTS = 4, 4
TILES = 4
AHEAD = 4

NO_NODE = 1 << 20
LOWEST = -3.0e38
ACCW = F + HEADS + 1

F32 = mybir.dt.float32
I32 = mybir.dt.int32
ALU = mybir.AluOpType
ACT = mybir.ActivationFunctionType
AX = mybir.AxisListType


def at_least(eng, sem, value):
    if isinstance(value, int) and value <= 0:
        return
    eng.wait_ge(sem, value)


def staged(eng, count, unroll, stages, setup=None):
    most = max(lead for lead, _ in stages)
    first, rounds = unroll, (count - most) // unroll

    def peeled(i):
        values = setup(i, 1) if setup and i >= 0 else None
        for lead, body in stages:
            s = i + lead
            if 0 <= s < count:
                body(s, s % unroll, s // unroll, *([values[0]] if setup and lead == 0 else []))

    for i in range(-most, first):
        peeled(i)
    with eng.Fori(1, rounds) as r:
        values = setup(r * unroll, unroll) if setup else None
        for j in range(unroll):
            for lead, body in stages:
                body(r * unroll + (j + lead), (j + lead) % unroll, r + (j + lead) // unroll,
                     *([values[j]] if setup and lead == 0 else []))
    for i in range(rounds * unroll, count):
        peeled(i)


def slot_free(eng, sem, r):
    if isinstance(r, int) and r == 0:
        return
    eng.wait_ge(sem, 16 * r)


def graph_layers(nc, x, src, dst, rel, weight1, Wq, Wk, Wv, Wscale, W1, b1, W2, gate2, W3, out):
    ctx = ExitStack()
    with ctx:
        def sb(name, shape, dt=F32):
            return ctx.enter_context(nc.sbuf_tensor(name, shape, dt))

        def sem(name):
            return ctx.enter_context(nc.semaphore(name))

        def sems(name, n):
            return [sem(f"{name}{i}") for i in range(n)]

        def dram(name, shape, dt=F32):
            return nc.dram_tensor(name, shape, dt).ap()

        win_d = dram("win_d", (STEPS,), I32)
        tile_d = dram("tile_d", (EXTRA,), I32)
        rows_d = dram("rows_d", (EDGE_TILES, 4 * P))
        dst_d = dram("dst_d", (GROUPS * ROW + 2,), I32)
        qv_d = dram("qv_d", (NPAD, 2 * F))
        v_d = dram("v_d", (P, STEPS, F))
        t1_d = dram("t1_d", (NPAD, F + 1))
        t2_d = dram("t2_d", (NPAD * RELS, F))
        t3_d = dram("t3_d", (NPAD * RELS, F))

        X = sb("X", [P, NODE_TILES, F])
        H = sb("H", [P, NODE_TILES, F])
        SUMS = sb("SUMS", [P, NODE_TILES, ACCW])
        big = sb("big", [P, 2 * ROW])
        rows = sb("rows", [P, 2 * (ROW + 2)])
        col = sb("col", [P, 4, STEPS])
        SW = sb("SW", [P, STEPS, HEADS + 1])
        ring = sb("ring", [P, RING, 2 * F])
        idx = sb("idx", [P, RING], I32)
        onehot = sb("onehot", [P, RING, P])
        onehotT = sb("onehotT", [P, BANKS, P])
        prod = sb("prod", [P, 2, F])
        vw = sb("vw", [P, RING, ACCW])
        hs = sb("hs", [P, TILES, F])
        hT = sb("hT", [P, TILES, F])
        wraw = sb("wraw", [P, 4, F])
        wsraw = sb("wsraw", [P, HEADS, F])
        wqkvT = sb("wqkvT", [P, 3 * F])
        wsT = sb("wsT", [P, F])
        w1T = sb("w1T", [P, F])
        w2 = sb("w2", [P, RELS, F])
        w3 = sb("w3", [P, RELS, F])
        g2 = sb("g2", [P, RELS])
        bias = sb("bias", [P, F])
        iota_row = sb("iota_row", [P, P])
        iota_col = sb("iota_col", [P, 1])
        next_row = sb("next_row", [P, EXTRA])
        next_col = sb("next_col", [P, 1])
        ident = sb("ident", [P, P])
        one = sb("one", [1, 2])
        win = sb("win", [1, STEPS], I32)
        tile = sb("tile", [1, EXTRA], I32)
        ends = sb("ends", [P, CHUNKS], I32)
        few = sb("few", [P, 8], I32)
        fewf = sb("fewf", [P, 8])
        xrows = sb("xrows", [P, 4 * P])
        stats = sb("stats", [P, NODE_TILES, 6])
        ln = sb("ln", [P, 4, NODE_TILES])
        rstd = sb("rstd", [P, NODE_TILES])
        shift = sb("shift", [P, NODE_TILES])
        rden = sb("rden", [P, NODE_TILES, HEADS])
        dinv = sb("dinv", [P, NODE_TILES])
        dtmp = sb("dtmp", [P, 2, NODE_TILES])
        carry = sb("carry", [P, 4])
        crow = sb("crow", [1, 4, P + 1])
        gate = sb("gate", [P, TILES, 2, RELS])
        minus1 = sb("minus1", [1, 4], I32)

        K = big[:, 0:NODE_TILES * F].rearrange("p (t f) -> p t f", f=F)
        ST = big[:, 0:ROW]
        FT = big[:, ROW:2 * ROW]
        RI = rows[:, 0:CHUNKS * 3 * P].bitcast(I32).rearrange("p (c k i) -> p c k i", c=CHUNKS, k=3)
        R = big[:, 0:CHUNKS * 4 * P].rearrange("p (c k i) -> p c k i", c=CHUNKS, k=4)
        spare = rows[:, CHUNKS * 3 * P:CHUNKS * 3 * P + 3 * EDGE_TILES].rearrange("p (k e) -> p k e", k=3)
        winb_i = spare[:, 0, :].bitcast(I32)
        winb = spare[:, 1, :]
        below = spare[:, 2, :]
        Tst = big[:, 0:NODE_TILES * (F + 1)].rearrange("p (t f) -> p t f", f=F + 1)
        drow = rows[:, 0:ROW + 2].bitcast(I32)
        MT = rows[:, 0:ROW]
        pen = rows[:, ROW + 2:2 * ROW + 2]
        y, hb = wraw, wsraw
        assert TILES == HEADS
        vin = ring[:].rearrange("p r (two f) -> p (r two) f", two=2)
        qv_out = rows[:, ROW + 2:ROW + 2 + TILES * 2 * F].rearrange("p (k f) -> p k f", k=TILES)
        rel_out = rows[:, 0:TILES * RELS * F].rearrange("p (k f) -> p k f", k=TILES)

        ps = [ctx.enter_context(nc.psum_tensor(f"ps{i}", [P, 512], F32)) for i in range(8)]

        s_const = sem("s_const")
        s_edges = sem("s_edges")
        s_x = sem("s_x")
        s_w = sem("s_w")
        s_scratch = sem("s_scratch")
        s_extra = sem("s_extra")
        dve_step = sem("dve_step")
        act_step = sem("act_step")
        pe_prep = sem("pe_prep")
        s_dpad = sem("s_dpad")
        s_drow = sem("s_drow")
        s_out = sem("s_out")
        s_issued = sem("s_issued")
        s_mid_pe = sem("s_mid_pe")
        s_mid_cp = sem("s_mid_cp")
        s_back_pe = sem("s_back_pe")
        s_back_cp = sem("s_back_cp")
        s_fold = sem("s_fold")

        q0 = dict(idx=sem("q0_idx"), rows=sems("q0_rows", RING), onehot=sem("q0_onehot"),
                             turned=sem("q0_turned"), copied=sem("q0_copied"), kexp=sem("q0_kexp"),
                             prod=sem("q0_prod"), score=sem("q0_score"), saved=sems("q0_saved", RING))
        a0 = dict(loaded=sems("a0_loaded", VSLOTS), vw=sem("a0_vw"), wcol=sem("a0_wcol"),
                             onehot=sem("a0_onehot"), summed=sem("a0_summed"), added=sem("a0_added"))

        def gsems(name):
            return dict(idx=sem(name + "_idx"), rows=sems(name + "_rows", RING),
                                   onehot=sem(name + "_onehot"), summed=sem(name + "_summed"),
                                   added=sem(name + "_added"))

        g1, gr2, gr3 = gsems("g1"), gsems("g2"), gsems("g3")

        def dsems(name, *more):
            s = {k: sem(f"{name}_{k}") for k in more}
            if name[0] == "d":
                s["stored"] = sems(name + "_stored", TILES)
            return s

        d0 = dsems("d0", "ln", "h", "xadd", "turned", "hT", "prod", "qv", "k")
        d2 = dsems("d2", "ln", "h", "turned", "hT", "gate", "gexp", "gone", "gsig", "prod", "dve", "act")
        d3 = dsems("d3", "ln", "h", "xadd", "turned", "hT", "prod", "dve", "act")
        p0 = dsems("p0", "inn", "turned", "T", "prod", "x", "stats")
        p1 = dsems("p1", "inn", "turned", "T", "prod", "hb", "y", "z", "x", "stats")
        p2 = dsems("p2", "stats")
        ln0 = dsems("ln0", "stats")
        s_t1d = sem("s_t1d")
        s_lnsq = sem("s_lnsq")
        s_dq = sem("s_dq")
        s_h1 = sem("s_h1")

        block = ctx.enter_context(nc.Block())

        mark = {}

        @block.vector
        def _(v):
            count = [0]

            def link(ins, name=None):
                count[0] += 1
                ins.then_inc(dve_step, 1)
                v.wait_ge(dve_step, count[0])
                if name:
                    mark[name] = count[0]

            win_regs = [v.alloc_register(f"win{k}") for k in range(RING)]
            tile_regs = [v.alloc_register(f"tile{k}") for k in range(RING)]

            def windows(s, n):
                v.reg_load(win_regs[0:n], win[0:1, bass.ds(s, n)])
                return [v.snap(r, min_val=0, max_val=NODE_TILES - 1) for r in win_regs[0:n]]

            def edge_tiles(s, n):
                v.reg_load(tile_regs[0:n], tile[0:1, bass.ds(s, n)])
                return [v.snap(r, min_val=0, max_val=EDGE_TILES - 1) for r in tile_regs[0:n]]

            v.wait_ge(s_const, 1)
            link(v.tensor_scalar(ident[:], iota_row[:], iota_col[:, 0:1], None, ALU.is_equal), "ident")
            v.wait_ge(s_edges, 12 * 16)
            link(v.tensor_scalar(ends[:], RI[:, :, 0, P - 1], 7, None, ALU.arith_shift_right), "ends")
            link(v.tensor_copy(R[:, :, 0:2, :], RI[:, :, 0:2, :]))
            link(v.scalar_tensor_tensor(R[:, :, 2, :], RI[:, :, 1, :], float(RELS), RI[:, :, 2, :],
                                        ALU.mult, ALU.add), "rows")
            v.wait_ge(s_scratch, 16 * 8)
            link(v.tensor_copy(winb[:], winb_i[:]))
            link(v.tensor_scalar(below[0:EXTRA, 0:EDGE_TILES - 1], winb[0:EXTRA, 1:EDGE_TILES],
                                 next_col[0:EXTRA, 0:1], None, ALU.is_lt))
            link(v.tensor_reduce(fewf[0:EXTRA, 0:1], below[0:EXTRA, 0:EDGE_TILES - 1], AX.X, ALU.add))
            link(v.tensor_copy(few[0:EXTRA, 0:1], fewf[0:EXTRA, 0:1]), "tiles")
            for c in range(CHUNKS + 1):
                w = P if c < CHUNKS - 1 else CTAIL if c == CHUNKS - 1 else EXTRA
                v.wait_ge(pe_prep, c + 1)
                o = c * P if c < CHUNKS else EDGE_TILES
                link(v.tensor_copy(col[:, :, o:o + w],
                                   ps[c][:].rearrange("p (k i) -> p k i", k=4)[:, :, 0:w]), f"col{c}")
            link(v.scalar_tensor_tensor(col[:, 0, 0:EDGE_TILES], winb[:], -float(P), col[:, 0, 0:EDGE_TILES],
                                        ALU.mult, ALU.add))
            link(v.scalar_tensor_tensor(col[:, 0, EDGE_TILES:STEPS], next_row[:], -float(P),
                                        col[:, 0, EDGE_TILES:STEPS], ALU.mult, ALU.add), "cols")
            v.wait_ge(s_w, 16 * 9)
            link(v.tensor_reduce(hs[:, 0, :], wsraw[:].rearrange("p h c -> p c h"), AX.X, ALU.add), "wsum")
            v.wait_ge(pe_prep, CHUNKS + 2)
            link(v.tensor_scalar(wqkvT[:, 0:F], ps[0][:, 0:F], HDIM ** -0.5, None, ALU.mult))
            link(v.tensor_copy(wqkvT[:, F:2 * F], ps[0][:, 2 * F:3 * F]))
            link(v.tensor_copy(wqkvT[:, 2 * F:3 * F], ps[0][:, F:2 * F]))
            link(v.tensor_copy(w1T[:], ps[0][:, 3 * F:4 * F]))
            link(v.tensor_copy(wsT[:], ps[1][:, 0:F]), "weights")

            def norm_stats(done):
                me, qe, mo, qo = (stats[:, :, j] for j in (1, 2, 4, 5))
                v.wait_ge(done, NODE_TILES)
                link(v.tensor_tensor(ln[:, 0, :], me, mo, ALU.add))
                link(v.tensor_tensor(ln[:, 1, :], me, mo, ALU.subtract))
                link(v.tensor_tensor(ln[:, 2, :], qe, qo, ALU.add))
                link(v.tensor_tensor(ln[:, 1, :], ln[:, 1, :], ln[:, 1, :], ALU.mult))
                link(v.tensor_scalar(ln[:, 2, :], ln[:, 2, :], 1.0 / F, EPS, ALU.mult, ALU.add))
                link(v.scalar_tensor_tensor(ln[:, 3, :], ln[:, 1, :], 0.25, ln[:, 2, :], ALU.mult, ALU.add),
                     f"var{len([m for m in mark if m.startswith('var')])}")

            def norm_scale(n):
                v.wait_ge(s_lnsq, n + 1)
                link(v.reciprocal(rstd[:], ln[:, 3, :]))
                link(v.scalar_tensor_tensor(shift[:], ln[:, 0, :], -0.5, rstd[:], ALU.mult, ALU.mult), f"ln{n}")

            v.wait_ge(s_x, 32)
            staged(v, NODE_TILES, TILES, [(0, lambda s, k, r: v.bn_stats(
                stats[:, bass.ds(s, 1), :], X[:, bass.ds(s, 1), :]).then_inc(ln0["stats"], 1))])
            norm_stats(ln0["stats"])
            norm_scale(0)

            def hT_copy(d):
                def body(s, k, r):
                    v.wait_ge(d["turned"], s + 1)
                    at_least(v, d["prod"], s - TILES + 1)
                    v.tensor_copy(hT[:, k, :], ps[k % 2][:, 0:F]).then_inc(d["hT"], 1)
                return body

            def d0_k(s, k, r):
                v.wait_ge(d0["prod"], s + 1)
                v.tensor_copy(K[:, bass.ds(s, 1), :],
                              ps[4 + k % 2][:, 0:F].rearrange("p (a f) -> p a f", a=1)).then_inc(d0["k"], 1)

            staged(v, NODE_TILES, TILES, [(2, hT_copy(d0)), (0, d0_k)])

            def build(s, k, done, value, sig, weighted=False):
                at_least(v, done, value)
                v.tensor_scalar(onehot[:, k, :], iota_row[:], col[:, 0, bass.ds(s, 1)],
                                col[:, 3, bass.ds(s, 1)] if weighted else None, ALU.is_equal,
                                **({"op1": ALU.mult} if weighted else {})).then_inc(sig, 1)

            v.wait_ge(d0["k"], NODE_TILES)

            def q0_build(s, k, r):
                build(s, k, q0["turned"], s - RING + 1, q0["onehot"])

            def q0_prod(s, k, r):
                v.wait_ge(q0["rows"][k], 16 * (r + 1))
                v.wait_ge(q0["kexp"], s + 1)
                at_least(v, q0["score"], s - 1)
                v.tensor_tensor(prod[:, k % 2, :], ring[:, k, 0:F], ps[4 + k % BANKS][:, 0:F],
                                ALU.mult).then_inc(q0["prod"], 1)

            def q0_sum(s, k, r):
                v.wait_ge(q0["prod"], s + 1)
                v.tensor_reduce(SW[:, bass.ds(s, 1), 0:HEADS],
                                prod[:, k % 2, :].rearrange("p (a h d) -> p a h d", a=1, h=HEADS),
                                AX.X, ALU.add).then_inc(q0["score"], 1)

            staged(v, STEPS, RING, [(AHEAD + 1, q0_build), (1, q0_prod), (0, q0_sum)])
            v.wait_ge(q0["score"], STEPS)

            def fold(s, e, j):
                at_least(v, s_fold, s)
                v.tensor_tensor(SW[:, bass.ds(e, 1), 0:HEADS], SW[:, bass.ds(e, 1), 0:HEADS],
                                SW[:, bass.ds(s + EDGE_TILES, 1), 0:HEADS], ALU.add).then_inc(s_fold, 1)

            v.wait_ge(s_scratch, 16 * 10)
            e = edge_tiles(0, RING)
            for k in range(RING):
                fold(k, e[k], k)
            with v.Fori(1, EXTRA // RING) as r:
                e = edge_tiles(r * RING, RING)
                for k in range(RING):
                    fold(r * RING + k, e[k], k)

            SWt = SW[:, 0:GROUPS * BLOCKS, 0:HEADS].rearrange("p (g b) h -> p b h g", b=BLOCKS)
            v.wait_ge(s_fold, EXTRA)
            link(v.tensor_copy(FT.rearrange("p (b h g) -> p b h g", b=BLOCKS, h=HEADS), SWt), "blocks")
            for b in range(0, BLOCKS, 4):
                n = min(4, BLOCKS - b)
                v.wait_ge(s_mid_pe, b // 4 + 1)
                v.tensor_copy(ST[:, b * P:(b + n) * P], ps[(b // 4) % 2][:, 0:n * P]).then_inc(s_mid_cp, 1)
            v.wait_ge(s_mid_cp, -(-BLOCKS // 4))
            v.wait_ge(s_drow, 64)
            link(v.tensor_tensor(pen[:], drow[:, 1:ROW + 1], drow[:, 0:ROW], ALU.not_equal))
            link(v.tensor_scalar(pen[:], pen[:], LOWEST, None, ALU.mult))
            link(v.tensor_tensor_scan(FT, pen, ST, LOWEST, ALU.add, ALU.max))
            link(v.tensor_tensor(carry[:, 0:1], drow[:, ROW:ROW + 1], drow[:, 0:1], ALU.not_equal))
            link(v.tensor_scalar(carry[:, 1:2], carry[:, 0:1], LOWEST, None, ALU.mult))
            link(v.tensor_copy(carry[:, 0:1], FT[:, ROW - 1:ROW]), "carry_f")
            v.wait_ge(s_mid_pe, -(-BLOCKS // 4) + 1)
            link(v.tensor_copy(crow[:, 0:2, 1:P + 1], ps[2][0:1, 0:2 * P].rearrange("p (k i) -> p k i", k=2)))
            link(v.tensor_tensor_scan(crow[:, 2, 1:P + 1], crow[:, 1, 1:P + 1], crow[:, 0, 1:P + 1],
                                      LOWEST, ALU.add, ALU.max))
            link(v.memset(crow[:, 2, 0:1], LOWEST), "crow_f")
            v.wait_ge(s_mid_pe, -(-BLOCKS // 4) + 2)
            link(v.tensor_copy(carry[:, 2:3], ps[3][:, 0:1]))
            link(v.tensor_tensor_scan(FT, pen, ST, carry[:, 2:3], ALU.add, ALU.max))
            link(v.tensor_tensor(pen[:], drow[:, 1:ROW + 1], drow[:, 2:ROW + 2], ALU.not_equal))
            link(v.tensor_scalar(pen[:], pen[:], LOWEST, None, ALU.mult))
            link(v.tensor_tensor(carry[:, 0:1], drow[:, 1:2], drow[:, ROW + 1:ROW + 2], ALU.not_equal))
            link(v.tensor_scalar(carry[:, 1:2], carry[:, 0:1], LOWEST, None, ALU.mult))
            link(v.tensor_tensor_scan(MT[:, ::-1], pen[:, ::-1], FT[:, ::-1], LOWEST, ALU.add, ALU.max))
            link(v.tensor_copy(carry[:, 0:1], MT[:, 0:1]), "carry_b")
            v.wait_ge(s_mid_pe, -(-BLOCKS // 4) + 3)
            link(v.tensor_copy(crow[:, 0:2, 0:P], ps[4][0:1, 0:2 * P].rearrange("p (k i) -> p k i", k=2)))
            link(v.tensor_tensor_scan(crow[:, 2, 0:P][:, ::-1], crow[:, 1, 0:P][:, ::-1], crow[:, 0, 0:P][:, ::-1],
                                      LOWEST, ALU.add, ALU.max))
            link(v.memset(crow[:, 2, P:P + 1], LOWEST), "crow_b")
            v.wait_ge(s_mid_pe, -(-BLOCKS // 4) + 4)
            link(v.tensor_copy(carry[:, 3:4], ps[5][:, 0:1]))
            link(v.tensor_tensor_scan(MT[:, ::-1], pen[:, ::-1], FT[:, ::-1], carry[:, 3:4], ALU.add, ALU.max))
            link(v.tensor_tensor(FT, ST, MT, ALU.subtract), "diff")
            for b in range(BLOCKS):
                v.wait_ge(s_back_pe, b + 1)
                v.tensor_copy(SWt[:, b], ps[b % 4][:, 0:P].rearrange("p (h g) -> p h g", h=HEADS)).then_inc(s_back_cp, 1)
            v.wait_ge(s_back_cp, BLOCKS)

            def spread(s, e, j):
                v.tensor_copy(SW[:, bass.ds(s + EDGE_TILES, 1), :], SW[:, bass.ds(e, 1), :]).then_inc(s_fold, 1)

            with v.Fori(0, EXTRA // RING) as r:
                e = edge_tiles(r * RING, RING)
                for k in range(RING):
                    spread(r * RING + k, e[k], k)
            v.wait_ge(s_fold, 2 * EXTRA)
            link(v.memset(SUMS[:], 0.0), "weights0")

            def add(s, bank, w, width, g):
                v.wait_ge(g["summed"], s + 1)
                at_least(v, g["added"], s)
                v.tensor_tensor(SUMS[:, bass.ds(w, 1), 0:width], SUMS[:, bass.ds(w, 1), 0:width],
                                ps[bank][:, 0:width].rearrange("p (a f) -> p a f", a=1), ALU.add).then_inc(g["added"], 1)

            def sum_pass(g, width, weighted):
                staged(v, STEPS, RING,
                       [(AHEAD, lambda s, k, r: build(s, k, g["summed"], s - RING + 1, g["onehot"], weighted)),
                        (0, lambda s, k, r, w: add(s, k, w, width, g))], setup=windows)
                v.wait_ge(g["added"], STEPS)

            sum_pass(a0, ACCW, False)
            SUMh = SUMS[:, :, 0:F]
            den = SUMS[:, :, F:F + HEADS]
            deg = SUMS[:, :, F + HEADS]
            link(v.scalar_tensor_tensor(rden[:], den, 0.0, den, ALU.is_equal, ALU.add))
            link(v.reciprocal(rden[:], rden[:]))
            link(v.scalar_tensor_tensor(dtmp[:, 0, :], deg, 0.0, deg, ALU.is_equal, ALU.add), "deg")

            def p0_in(s, k, r):
                at_least(v, p0["turned"], s - TILES + 1)
                v.tensor_tensor(hs[:, k, :].rearrange("p (h d) -> p h d", h=HEADS),
                                SUMS[:, bass.ds(s, 1), 0:F].rearrange("p a (h d) -> p (a h) d", h=HEADS),
                                rden[:, bass.ds(s, 1), :].rearrange("p a h -> p (a h)").unsqueeze(2).to_broadcast([P, HEADS, HDIM]),
                                ALU.mult).then_inc(p0["inn"], 1)

            def p0_add(s, k, r):
                v.wait_ge(p0["prod"], s + 1)
                v.tensor_tensor(X[:, bass.ds(s, 1), :], X[:, bass.ds(s, 1), :],
                                ps[4 + k][:, 0:F].rearrange("p (a f) -> p a f", a=1), ALU.add).then_inc(p0["x"], 1)

            def tile_stats(p):
                def body(s, k, r):
                    v.wait_ge(p["x"], s + 1)
                    v.bn_stats(stats[:, bass.ds(s, 1), :], X[:, bass.ds(s, 1), :]).then_inc(p["stats"], 1)
                return body

            v.wait_ge(d0["xadd"], NODE_TILES)
            staged(v, NODE_TILES, TILES, [(4, p0_in), (1, p0_add), (0, tile_stats(p0))])
            norm_stats(p0["stats"])
            norm_scale(1)
            v.wait_ge(s_dq, 1)
            link(v.reciprocal(dtmp[:, 1, :], dtmp[:, 0, :]))
            link(v.scalar_tensor_tensor(dinv[:], deg, 0.0, dtmp[:, 1, :], ALU.is_gt, ALU.mult))

            v.wait_ge(s_h1, NODE_TILES)
            link(v.tensor_copy(Tst[:, :, F], dinv[:]))
            link(v.tensor_tensor(Tst[:, :, 0:F], H[:], dinv[:].unsqueeze(2).to_broadcast([P, NODE_TILES, F]),
                                 ALU.mult), "t1")
            link(v.memset(SUMS[:], 0.0))
            sum_pass(g1, F + 1, False)

            def p1_in(s, k, r):
                at_least(v, p1["turned"], s - TILES + 1)
                v.tensor_tensor(hs[:, k, :].rearrange("p (a f) -> p a f", a=1), SUMS[:, bass.ds(s, 1), 0:F],
                                H[:, bass.ds(s, 1), :], ALU.mult).then_inc(p1["inn"], 1)

            def p1_y(s, k, r):
                v.wait_ge(p1["prod"], s + 1)
                v.wait_ge(p1["hb"], s + 1)
                v.scalar_tensor_tensor(y[:, k, :], hb[:, k, :], SUMS[:, bass.ds(s, 1), F:F + 1].rearrange("p a b -> p (a b)"),
                                       ps[4 + k][:, 0:F], ALU.mult, ALU.add).then_inc(p1["y"], 1)

            def p1_z(s, k, r):
                v.wait_ge(p1["y"], s + 1)
                v.scalar_tensor_tensor(y[:, k, :], y[:, k, :], SLOPE, y[:, k, :], ALU.mult, ALU.max).then_inc(p1["z"], 1)

            def p1_x(s, k, r):
                v.wait_ge(p1["z"], s + 1)
                v.scalar_tensor_tensor(X[:, bass.ds(s, 1), :], y[:, k, :].rearrange("p (a f) -> p a f", a=1),
                                       dinv[:, bass.ds(s, 1)], X[:, bass.ds(s, 1), :], ALU.mult, ALU.add).then_inc(p1["x"], 1)

            staged(v, NODE_TILES, TILES, [(6, p1_in), (3, p1_y), (2, p1_z), (1, p1_x), (0, tile_stats(p1))])
            norm_stats(p1["stats"])
            norm_scale(2)

            half = RELS // 2 * F

            def d2_add(s, k, r):
                v.wait_ge(d2["gexp"], s + 1)
                v.tensor_scalar(gate[:, k, 1, :], gate[:, k, 0, :], 1.0, None, ALU.add).then_inc(d2["gone"], 1)

            def d2_gate(s, k, r):
                v.wait_ge(d2["gone"], s + 1)
                at_least(v, d2["act"], s - TILES + 1)
                v.reciprocal(gate[:, k, 0, :], gate[:, k, 1, :]).then_inc(d2["gsig"], 1)

            def d2_out(s, k, r):
                v.wait_ge(d2["gsig"], s + 1)
                v.wait_ge(d2["prod"], s + 1)
                slot_free(v, d2["stored"][k], r)
                v.tensor_tensor(rel_out[:, k, 0:half].rearrange("p (q f) -> p q f", f=F),
                                ps[4 + 2 * (k % 2)][:].rearrange("p (q f) -> p q f", f=F),
                                gate[:, k, 0, 0:RELS // 2].unsqueeze(2).to_broadcast([P, RELS // 2, F]),
                                ALU.mult).then_inc(d2["dve"], 1)

            staged(v, NODE_TILES, TILES, [(2, hT_copy(d2)), (1, d2_add), (1, d2_gate), (0, d2_out)])
            link(v.memset(SUMS[:], 0.0))
            sum_pass(gr2, F, True)
            link(v.scalar_tensor_tensor(X[:], SUMh, 0.0, X[:], ALU.max, ALU.add))
            staged(v, NODE_TILES, TILES, [(0, lambda s, k, r: v.bn_stats(
                stats[:, bass.ds(s, 1), :], X[:, bass.ds(s, 1), :]).then_inc(p2["stats"], 1))])
            norm_stats(p2["stats"])
            norm_scale(3)

            def d3_out(s, k, r):
                v.wait_ge(d3["prod"], s + 1)
                slot_free(v, d3["stored"][k], r)
                v.tensor_copy(rel_out[:, k, 0:half], ps[4 + 2 * (k % 2)][:]).then_inc(d3["dve"], 1)

            staged(v, NODE_TILES, TILES, [(2, hT_copy(d3)), (0, d3_out)])
            link(v.memset(SUMS[:], 0.0))
            sum_pass(gr3, F, False)
            v.wait_ge(d3["xadd"], NODE_TILES)
            link(v.tensor_tensor(X[:], SUMh, X[:], ALU.add), "final")

        @block.gpsimd
        def _(g):
            g.iota(iota_row[:], [[1, P]], base=0, channel_multiplier=0, allow_small_or_imprecise_dtypes=True)
            g.iota(iota_col[:], [[0, 1]], base=0, channel_multiplier=1, allow_small_or_imprecise_dtypes=True)
            g.iota(next_row[:], [[1, EXTRA]], base=1, channel_multiplier=0, allow_small_or_imprecise_dtypes=True)
            g.iota(next_col[:], [[0, 1]], base=1, channel_multiplier=1, allow_small_or_imprecise_dtypes=True)
            g.memset(X[:, NODE_TILES - 1, :], 0.0)
            g.memset(RI[:, :, 0, :], NO_NODE)
            g.memset(RI[:, :, 1:3, :], 0)
            g.memset(R[:, :, 3, :], 0.0)
            g.memset(one[:], 1.0)
            g.memset(minus1[:, 0:1], -1)
            g.memset(minus1[:, 1:2], NO_NODE)
            g.memset(minus1[:, 2:3], 0)
            g.memset(SW[:], 1.0)
            g.iota(tile[:], [[1, EXTRA]], base=1, channel_multiplier=0).then_inc(s_const, 1)

            g.wait_ge(dve_step, mark["tiles"])
            g.wait_ge(s_scratch, 16 * 6)
            g.indirect_dma_start(xrows[0:EXTRA, :], None, rows_d[:, :],
                                 bass.IndirectOffsetOnAxis(ap=few[0:EXTRA, 0:1], axis=0)).then_inc(s_extra, 16)

            def xadd(d, s, k):
                g.wait_ge(d["h"], s + 1)
                g.tensor_tensor(X[:, bass.ds(s, 1), :], X[:, bass.ds(s, 1), :],
                                hs[:, k, :].rearrange("p (a f) -> p a f", a=1), ALU.add).then_inc(d["xadd"], 1)

            staged(g, NODE_TILES, TILES, [(0, lambda s, k, r: xadd(d0, s, k))])

            def table_waits(d):
                return [(d["stored"][k], 16 * len(range(k, NODE_TILES, TILES))) for k in range(TILES)]

            def gather(q, table, width, freed, written):
                def body(s, k, r):
                    for name, free in freed:
                        if name == "step":
                            at_least(g, free, s - RING + 1)
                        else:
                            slot_free(g, free[k], r)
                    for d, n in written:
                        g.wait_ge(d, n)
                    g.wait_ge(q["idx"], s + 1)
                    g.sem_inc(s_issued, 1)
                    g.indirect_dma_start(ring[:, k, 0:width], None, table,
                                         bass.IndirectOffsetOnAxis(ap=idx[:, k:k + 1], axis=0)).then_inc(q["rows"][k], 16)
                staged(g, STEPS, RING, [(0, body)])

            table_done = table_waits(d0)
            gather(q0, qv_d[:, :], 2 * F, [("step", q0["prod"]), ("slot", q0["saved"])], table_done)

            g.wait_ge(dve_step, mark["weights0"])

            def weigh(s, k, r):
                g.wait_ge(a0["loaded"][k // VB], 16 * (r + 1))
                at_least(g, a0["summed"], s - RING + 1)
                g.tensor_tensor(vw[:, k % RING, 0:F].rearrange("p (h d) -> p h d", h=HEADS),
                                vin[:, k, :].rearrange("p (h d) -> p h d", h=HEADS),
                                SW[:, bass.ds(s, 1), 0:HEADS].rearrange("p a h -> p (a h)").unsqueeze(2).to_broadcast([P, HEADS, HDIM]),
                                ALU.mult).then_inc(a0["vw"], 1)

            staged(g, STEPS, VB * VSLOTS, [(0, weigh)])

            gather(g1, t1_d[:, :], F + 1, [("step", g1["summed"])], [(s_t1d, 16)])

            def add_bias(s, k, r):
                at_least(g, p1["y"], s - TILES + 1)
                g.tensor_tensor(hb[:, k, :].rearrange("p (a f) -> p a f", a=1), H[:, bass.ds(s, 1), :],
                                bias[:].rearrange("p (a f) -> p a f", a=1), ALU.add).then_inc(p1["hb"], 1)

            staged(g, NODE_TILES, TILES, [(0, add_bias)])
            table_done = table_waits(d2)
            gather(gr2, t2_d[:, :], F, [("step", gr2["summed"])], table_done)
            staged(g, NODE_TILES, TILES, [(0, lambda s, k, r: xadd(d3, s, k))])
            table_done = table_waits(d3)
            gather(gr3, t3_d[:, :], F, [("step", gr3["summed"])], table_done)

        @block.scalar
        def _(a):
            def root(n):
                a.wait_ge(dve_step, mark[f"var{n}"])
                a.activation(ln[:, 3, :], ln[:, 3, :], ACT.Sqrt).then_inc(s_lnsq, 1)

            def normed(d):
                def body(s, k, r):
                    at_least(a, d["turned"], s - TILES + 1)
                    if "xadd" in d:
                        at_least(a, d["xadd"], s - TILES + 1)
                    a.activation(hs[:, k, :].rearrange("p (a f) -> p a f", a=1), X[:, bass.ds(s, 1), :], ACT.Relu,
                                 bias=shift[:, bass.ds(s, 1)], scale=rstd[:, bass.ds(s, 1)]).then_inc(d["h"], 1)
                return body

            root(0)
            a.wait_ge(dve_step, mark["ln0"])

            def d0_out(s, k, r):
                a.wait_ge(d0["prod"], s + 1)
                slot_free(a, d0["stored"][k], r)
                a.activation(qv_out[:, k, :], ps[2 + k % 2][:, 0:2 * F], ACT.Copy).then_inc(d0["qv"], 1)

            staged(a, NODE_TILES, TILES, [(3, normed(d0)), (0, d0_out)])

            def index(q, kind):
                def body(s, k, r):
                    slot_free(a, q["rows"][k], r)
                    a.activation(idx[:, k:k + 1], col[:, kind, bass.ds(s, 1)], ACT.Copy).then_inc(q["idx"], 1)
                return body

            a.wait_ge(dve_step, mark["cols"])

            def q0_copy(s, k, r):
                a.wait_ge(q0["turned"], s + 1)
                at_least(a, q0["kexp"], s - BANKS + 1)
                a.activation(onehotT[:, k % BANKS, :], ps[k % BANKS][:, 0:P], ACT.Copy).then_inc(q0["copied"], 1)

            staged(a, STEPS, RING, [(2, q0_copy), (RING, index(q0, 1))])

            a.wait_ge(dve_step, mark["diff"])
            a.activation(ST, FT, ACT.Exp).then_inc(act_step, 1)

            a.wait_ge(dve_step, mark["weights0"])

            def wcol(s, k, r):
                at_least(a, a0["summed"], s - RING + 1)
                a.activation(vw[:, k, F:ACCW].rearrange("p (a f) -> p a f", a=1), SW[:, bass.ds(s, 1), :],
                             ACT.Copy).then_inc(a0["wcol"], 1)

            staged(a, STEPS, RING, [(0, wcol)])
            a.wait_ge(dve_step, mark["deg"])
            a.activation(dtmp[:, 0, :], dtmp[:, 0, :], ACT.Sqrt).then_inc(s_dq, 1)

            def turned_copy(p):
                def body(s, k, r):
                    a.wait_ge(p["turned"], s + 1)
                    at_least(a, p["prod"], s - TILES + 1)
                    a.activation(hT[:, k, :], ps[k][:, 0:F], ACT.Copy).then_inc(p["T"], 1)
                return body

            staged(a, NODE_TILES, TILES, [(0, turned_copy(p0))])
            root(1)
            a.wait_ge(dve_step, mark["ln1"])
            staged(a, NODE_TILES, TILES, [(0, lambda s, k, r: a.activation(
                H[:, bass.ds(s, 1), :], X[:, bass.ds(s, 1), :], ACT.Relu,
                bias=shift[:, bass.ds(s, 1)], scale=rstd[:, bass.ds(s, 1)]).then_inc(s_h1, 1))])

            staged(a, STEPS, RING, [(0, index(g1, 1))])
            staged(a, NODE_TILES, TILES, [(0, turned_copy(p1))])
            root(2)
            a.wait_ge(dve_step, mark["ln2"])

            half = RELS // 2

            def d2_exp(s, k, r):
                a.wait_ge(d2["gate"], s + 1)
                at_least(a, d2["dve"], s - TILES + 1)
                a.activation(gate[:, k, 0, :], ps[2 + k % 2][:, 0:RELS], ACT.Exp, scale=-1.0).then_inc(d2["gexp"], 1)

            def d2_out(s, k, r):
                a.wait_ge(d2["gsig"], s + 1)
                a.wait_ge(d2["prod"], s + 1)
                slot_free(a, d2["stored"][k], r)
                for q in range(half):
                    ins = a.activation(rel_out[:, k, (half + q) * F:(half + q + 1) * F],
                                       ps[5 + 2 * (k % 2)][:, q * F:(q + 1) * F], ACT.Copy,
                                       scale=gate[:, k, 0, half + q:half + q + 1])
                ins.then_inc(d2["act"], 1)

            staged(a, NODE_TILES, TILES, [(3, normed(d2)), (1, d2_exp), (0, d2_out)])
            staged(a, STEPS, RING, [(0, index(gr2, 2))])
            root(3)
            a.wait_ge(dve_step, mark["ln3"])

            def d3_out(s, k, r):
                a.wait_ge(d3["prod"], s + 1)
                slot_free(a, d3["stored"][k], r)
                a.activation(rel_out[:, k, half * F:RELS * F], ps[5 + 2 * (k % 2)][:], ACT.Copy).then_inc(d3["act"], 1)

            staged(a, NODE_TILES, TILES, [(3, normed(d3)), (0, d3_out)])
            staged(a, STEPS, RING, [(0, index(gr3, 2))])

        @block.tensor
        def _(t):
            win_regs = [t.alloc_register(f"pwin{k}") for k in range(RING)]

            def windows(s, n):
                t.reg_load(win_regs[0:n], win[0:1, bass.ds(s, n)])
                return [t.snap(r, min_val=0, max_val=NODE_TILES - 1) for r in win_regs[0:n]]

            t.wait_ge(dve_step, mark["rows"])
            t.wait_ge(s_edges, 12 * 16)
            for c in range(CHUNKS):
                n = P if c < CHUNKS - 1 else CTAIL
                for kind in range(4):
                    ins = t.transpose(ps[c][:, kind * P:kind * P + n], R[0:n, c, kind, :], ident[0:n, 0:n])
                ins.then_inc(pe_prep, 1)
            t.wait_ge(s_extra, 16)
            for kind in range(4):
                ins = t.transpose(ps[CHUNKS][:, kind * P:kind * P + EXTRA], xrows[0:EXTRA, kind * P:(kind + 1) * P],
                                  ident[0:EXTRA, 0:EXTRA])
            ins.then_inc(pe_prep, 1)
            t.wait_ge(s_w, 16 * 9)
            t.wait_ge(dve_step, mark["wsum"])
            for j in range(4):
                t.transpose(ps[0][:, j * F:(j + 1) * F], wraw[:, j, :], ident[:])
            t.transpose(ps[1][:, 0:F], hs[:, 0, :], ident[:]).then_inc(pe_prep, 1)

            def turn(d, source, copied, banks):
                def body(s, k, r):
                    t.wait_ge(d[source], s + 1)
                    at_least(t, d[copied], s - banks + 1)
                    t.transpose(ps[k % banks][:, 0:F], hs[:, k, :], ident[:]).then_inc(d["turned"], 1)
                return body

            t.wait_ge(dve_step, mark["weights"])

            def d0_prod(s, k, r):
                t.wait_ge(d0["hT"], s + 1)
                at_least(t, d0["qv"], s - 1)
                at_least(t, d0["k"], s - 1)
                t.matmul(ps[2 + k % 2][:, 0:2 * F], hT[:, k, :], wqkvT[:, 0:2 * F], start=True, stop=True)
                t.matmul(ps[4 + k % 2][:, 0:F], hT[:, k, :], wqkvT[:, 2 * F:3 * F], start=True, stop=True).then_inc(d0["prod"], 1)

            staged(t, NODE_TILES, TILES, [(2, turn(d0, "h", "hT", 2)), (0, d0_prod)])

            t.wait_ge(d0["k"], NODE_TILES)
            t.wait_ge(d0["qv"], NODE_TILES)
            t.wait_ge(s_scratch, 16 * 8)

            def q0_turn(s, k, r):
                t.wait_ge(q0["onehot"], s + 1)
                at_least(t, q0["copied"], s - BANKS + 1)
                t.transpose(ps[k % BANKS][:, 0:P], onehot[:, k, :], ident[:]).then_inc(q0["turned"], 1)

            def q0_kexp(s, k, r, w):
                t.wait_ge(q0["copied"], s + 1)
                at_least(t, q0["prod"], s - BANKS + 1)
                t.matmul(ps[4 + k % BANKS][:, 0:F], onehotT[:, k % BANKS, :], K[:, bass.ds(w, 1), :].rearrange("p a f -> p (a f)"),
                         start=True, stop=True).then_inc(q0["kexp"], 1)

            staged(t, STEPS, RING, [(3, q0_turn), (0, q0_kexp)], setup=windows)

            t.wait_ge(dve_step, mark["blocks"])
            n4 = -(-BLOCKS // 4)
            for b in range(0, BLOCKS, 4):
                at_least(t, s_mid_cp, b // 4 - 1)
                for j in range(min(4, BLOCKS - b)):
                    ins = t.transpose(ps[(b // 4) % 2][:, j * P:(j + 1) * P], FT[:, (b + j) * P:(b + j + 1) * P], ident[:])
                ins.then_inc(s_mid_pe, 1)
            for name, bank in (("f", 2), ("b", 4)):
                t.wait_ge(dve_step, mark["carry_" + name])
                t.transpose(ps[bank][0:1, 0:P], carry[:, 0:1], ident[:])
                t.transpose(ps[bank][0:1, P:2 * P], carry[:, 1:2], ident[:]).then_inc(s_mid_pe, 1)
                t.wait_ge(dve_step, mark["crow_" + name])
                o = 0 if name == "f" else 1
                t.matmul(ps[bank + 1][:, 0:1], crow[0:1, 2, o:o + P], one[0:1, 0:1], start=True, stop=True).then_inc(s_mid_pe, 1)
            t.wait_ge(act_step, 1)
            for b in range(BLOCKS):
                at_least(t, s_back_cp, b - 3)
                t.transpose(ps[b % 4][:, 0:P], ST[:, b * P:(b + 1) * P], ident[:]).then_inc(s_back_pe, 1)

            def a0_step(s, k, r):
                t.wait_ge(a0["onehot"], s + 1)
                t.wait_ge(a0["vw"], s + 1)
                t.wait_ge(a0["wcol"], s + 1)
                at_least(t, a0["added"], s - RING + 1)
                t.matmul(ps[k][:, 0:ACCW], onehot[:, k, :], vw[:, k, :], start=True, stop=True).then_inc(a0["summed"], 1)

            t.wait_ge(s_back_cp, BLOCKS)
            staged(t, STEPS, RING, [(0, a0_step)])

            def node_product(p, weight, free):
                def body(s, k, r):
                    t.wait_ge(p["T"], s + 1)
                    at_least(t, free, s - TILES + 1)
                    t.matmul(ps[4 + k][:, 0:F], hT[:, k, :], weight, start=True, stop=True).then_inc(p["prod"], 1)

                staged(t, NODE_TILES, TILES, [(2, turn(p, "inn", "T", 4)), (0, body)])

            t.wait_ge(a0["added"], STEPS)
            node_product(p0, wsT[:], p0["x"])

            def sum_step(g, width):
                def body(s, k, r):
                    t.wait_ge(g["onehot"], s + 1)
                    t.wait_ge(g["rows"][k], 16 * (r + 1))
                    at_least(t, g["added"], s - RING + 1)
                    t.matmul(ps[k][:, 0:width], onehot[:, k, :], ring[:, k, 0:width], start=True, stop=True).then_inc(g["summed"], 1)
                return body

            t.wait_ge(p0["x"], NODE_TILES)
            staged(t, STEPS, RING, [(0, sum_step(g1, F + 1))])
            t.wait_ge(g1["added"], STEPS)
            node_product(p1, w1T[:], p1["y"])

            def relations(d, w, gated):
                half = RELS // 2

                def gates(s, k, r):
                    t.wait_ge(d["hT"], s + 1)
                    at_least(t, d["gexp"], s - 1)
                    t.matmul(ps[2 + k % 2][:, 0:RELS], hT[:, k, :], g2[:], start=True, stop=True).then_inc(d["gate"], 1)

                def body(s, k, r):
                    t.wait_ge(d["hT"], s + 1)
                    at_least(t, d["dve"], s - 1)
                    at_least(t, d["act"], s - 1)
                    b = 4 + 2 * (k % 2)
                    t.matmul(ps[b][:], hT[:, k, :], w[:, 0:half, :].rearrange("p q f -> p (q f)"), start=True, stop=True)
                    t.matmul(ps[b + 1][:], hT[:, k, :], w[:, half:RELS, :].rearrange("p q f -> p (q f)"),
                             start=True, stop=True).then_inc(d["prod"], 1)

                staged(t, NODE_TILES, TILES, [(2, turn(d, "h", "hT", 2))] + [(1, gates)] * gated + [(0, body)])

            t.wait_ge(p1["y"], NODE_TILES)
            relations(d2, w2, True)
            t.wait_ge(d2["dve"], NODE_TILES)
            t.wait_ge(d2["act"], NODE_TILES)
            staged(t, STEPS, RING, [(0, sum_step(gr2, F))])
            t.wait_ge(gr2["added"], STEPS)
            relations(d3, w3, False)
            t.wait_ge(d3["dve"], NODE_TILES)
            t.wait_ge(d3["act"], NODE_TILES)
            staged(t, STEPS, RING, [(0, sum_step(gr3, F))])

        @block.sync
        def _(sp):
            full = (NODE_TILES - 1) * P
            sp.wait_ge(s_const, 1)
            sp.dma_start(X[:, 0:NODE_TILES - 1, :], x[0:full, :].rearrange("(t p) f -> p t f", p=P)).then_inc(s_x, 16)
            sp.dma_start(X[0:NTAIL, NODE_TILES - 1, :], x[full:N, :]).then_inc(s_x, 16)
            c6 = (CHUNKS - 1) * P * P
            tail = (EDGE_TILES - 1) * P
            for kind, a in ((0, dst), (1, src), (2, rel), (3, weight1)):
                t_ = R[:, :, 3, :] if kind == 3 else RI[:, :, kind, :]
                sp.dma_start(t_[:, 0:CHUNKS - 1, :], a[0:c6].rearrange("(c p i) -> p c i", p=P, i=P)).then_inc(s_edges, 16)
                sp.dma_start(t_[0:CTAIL - 1, CHUNKS - 1, :], a[c6:tail].rearrange("(p i) -> p i", i=P)).then_inc(s_edges, 16)
                sp.dma_start(t_[CTAIL - 1:CTAIL, CHUNKS - 1, 0:ETAIL], a[tail:E].rearrange("(a i) -> a i", a=1)).then_inc(s_edges, 16)
            for j, w in enumerate((Wq, Wk, Wv, W1)):
                sp.dma_start(wraw[:, j, :], w).then_inc(s_w, 16)
            sp.dma_start(wsraw[:], Wscale.rearrange("(h i) c -> i h c", h=HEADS)).then_inc(s_w, 16)
            sp.dma_start(w2[:], W2.rearrange("r d f -> d r f")).then_inc(s_w, 16)
            sp.dma_start(w3[:], W3.rearrange("r d f -> d r f")).then_inc(s_w, 16)
            sp.dma_start(g2[:], gate2.rearrange("r d o -> d (r o)"), allow_slow_non_contiguous=True).then_inc(s_w, 16)
            sp.dma_start(bias[:], bass.AP(b1.tensor, 0, [[0, P], [1, F]])).then_inc(s_w, 16)

            sp.wait_ge(dve_step, mark["rows"])
            nfull = (CHUNKS - 1) * P
            sp.dma_start(win_d[1:1 + nfull].rearrange("(c p) -> p c", p=P), ends[:, 0:CHUNKS - 1], allow_slow_non_contiguous=True).then_inc(s_scratch, 16)
            sp.dma_start(win_d[1 + nfull:EDGE_TILES].rearrange("(p a) -> p a", a=1),
                         ends[0:CTAIL - 1, CHUNKS - 1:CHUNKS]).then_inc(s_scratch, 16)
            sp.dma_start(win_d[0:1].rearrange("(a b) -> a b", a=1), minus1[:, 2:3]).then_inc(s_scratch, 16)
            sp.dma_start(win_d[EDGE_TILES:STEPS].rearrange("(a b) -> a b", a=1), tile[:]).then_inc(s_scratch, 16)
            sp.dma_start(rows_d[0:nfull, :].rearrange("(c p) f -> p c f", p=P),
                         R[:, 0:CHUNKS - 1].rearrange("p c k i -> p c (k i)")).then_inc(s_scratch, 16)
            sp.dma_start(rows_d[nfull:EDGE_TILES, :], R[0:CTAIL, CHUNKS - 1].rearrange("p k i -> p (k i)")).then_inc(s_scratch, 16)
            sp.dma_start(dst_d[1:1 + nfull * P].rearrange("(c p i) -> p c i", p=P, i=P), RI[:, 0:CHUNKS - 1, 0, :]).then_inc(s_dpad, 16)
            rest = GROUPS * BLOCKS - nfull
            sp.dma_start(dst_d[1 + nfull * P:1 + GROUPS * ROW].rearrange("(p i) -> p i", i=P), RI[0:rest, CHUNKS - 1, 0, :]).then_inc(s_dpad, 16)
            sp.dma_start(dst_d[0:1].rearrange("(a b) -> a b", a=1), minus1[:, 0:1]).then_inc(s_dpad, 16)
            sp.dma_start(dst_d[GROUPS * ROW + 1:GROUPS * ROW + 2].rearrange("(a b) -> a b", a=1), minus1[:, 1:2]).then_inc(s_dpad, 16)
            sp.wait_ge(s_scratch, 16 * 6)
            sp.dma_start(winb_i, bass.AP(win_d.tensor, 0, [[0, P], [1, EDGE_TILES]])).then_inc(s_scratch, 16)
            sp.dma_start(win[:], win_d.rearrange("(a b) -> a b", a=1)).then_inc(s_scratch, 16)
            sp.wait_ge(dve_step, mark["tiles"])
            sp.wait_ge(s_scratch, 16 * 8)
            sp.dma_start(tile_d.rearrange("(p a) -> p a", a=1), few[0:EXTRA, 0:1]).then_inc(s_scratch, 16)
            sp.wait_ge(s_scratch, 16 * 9)
            sp.dma_start(tile[:], tile_d.rearrange("(a b) -> a b", a=1)).then_inc(s_scratch, 16)
            sp.wait_ge(s_dpad, 64)
            sp.wait_ge(dve_step, mark["cols"])
            for h in range(HEADS):
                sp.dma_start(drow[h * GROUPS:(h + 1) * GROUPS, :],
                             bass.AP(dst_d.tensor, 0, [[ROW, GROUPS], [1, ROW + 2]])).then_inc(s_drow, 16)

            def store(d, table, staged_rows, waits):
                def body(s, k, r):
                    for w in waits:
                        sp.wait_ge(w, s + 1)
                    sp.dma_start(table[bass.ds(s * P, P), :], staged_rows[:, k, :]).then_inc(d["stored"][k], 16)
                staged(sp, NODE_TILES, TILES, [(0, body)])

            store(d0, qv_d, qv_out, [d0["qv"]])

            def save(s, k, r):
                sp.wait_ge(q0["rows"][k], 16 * (r + 1))
                sp.dma_start(v_d[:, bass.ds(s, 1), :], ring[:, k, F:2 * F].rearrange("p (a f) -> p a f", a=1)).then_inc(q0["saved"][k], 16)

            staged(sp, STEPS, RING, [(0, save)])
            for k in range(RING):
                sp.wait_ge(q0["saved"][k], 16 * (STEPS // RING + (k < STEPS % RING)))

            sp.wait_ge(q0["prod"], STEPS)

            def load(b, j, r):
                at_least(sp, a0["vw"], (b - VSLOTS + 1) * VB)
                sp.dma_start(vin[:, j * VB:(j + 1) * VB, :], v_d[:, bass.ds(b * VB, VB), :]).then_inc(a0["loaded"][j], 16)

            batches = STEPS // VB
            staged(sp, batches, VSLOTS, [(0, load)])
            j = batches % VSLOTS
            sp.wait_ge(a0["vw"], (batches - VSLOTS + 1) * VB)
            sp.dma_start(vin[:, j * VB:j * VB + STEPS % VB, :], v_d[:, batches * VB:STEPS, :]).then_inc(a0["loaded"][j], 16)

            sp.wait_ge(dve_step, mark["t1"])
            sp.dma_start(t1_d.rearrange("(t p) f -> p t f", p=P), Tst).then_inc(s_t1d, 16)
            store(d2, t2_d.rearrange("(n r) f -> n (r f)", r=RELS), rel_out, [d2["dve"], d2["act"]])
            store(d3, t3_d.rearrange("(n r) f -> n (r f)", r=RELS), rel_out, [d3["dve"], d3["act"]])
            sp.wait_ge(dve_step, mark["final"])
            sp.dma_start(out[0:full, :].rearrange("(t p) f -> p t f", p=P), X[:, 0:NODE_TILES - 1, :]).then_inc(s_out, 16)
            sp.dma_start(out[full:N, :], X[0:NTAIL, NODE_TILES - 1, :]).then_inc(s_out, 16)
            sp.wait_ge(s_out, 32)


_INS = ["x", "src", "dst", "edge_type_8", "edge_weight1", "L0_gnn_Wq", "L0_gnn_Wk", "L0_gnn_Wv", "L0_gnn_Wscale",
        "L1_gnn_W1_w", "L1_gnn_W1_b", "L2_gnn_weight", "L2_gnn_gate_weight", "L3_gnn_W"]


def kernel(**inputs):
    import numpy as np
    import concourse.bacc as bacc
    from concourse.bass_utils import run_bass_kernel_spmd

    nc = bacc.Bacc("TRN2", target_bir_lowering=False, num_devices=1)
    arrays, args = {}, []
    for name in _INS:
        a = np.ascontiguousarray(inputs[name])
        if name == "edge_weight1":
            a = a.reshape(-1)
        arrays["in_" + name] = a
        args.append(nc.dram_tensor("in_" + name, a.shape, mybir.dt.from_np(a.dtype), kind="ExternalInput").ap())
    out = nc.dram_tensor("out", (N, F), F32, kind="ExternalOutput").ap()
    graph_layers(nc, *args, out)
    return run_bass_kernel_spmd(nc, [arrays], core_ids=[0]).results[0]["out"]
```

```python
from contextlib import ExitStack

import concourse.bass as bass
from concourse import mybir

P = 128
N, E, F = 6250, 100000, 128
HEADS, HDIM = 4, 32
RELS = 8
EPS = 1e-5
SLOPE = 0.01

NODE_TILES = -(-N // P)
NPAD = NODE_TILES * P
NTAIL = N - (NODE_TILES - 1) * P
RING = 8
REAL_TILES = -(-E // P)
EDGE_TILES = -(-REAL_TILES // RING) * RING
ETAIL = E - (REAL_TILES - 1) * P
EXTRA = NODE_TILES - 1
STEPS = EDGE_TILES + EXTRA
CHUNKS = -(-EDGE_TILES // P)
CTAIL = EDGE_TILES - (CHUNKS - 1) * P
REAL_CTAIL = REAL_TILES - (CHUNKS - 1) * P

GROUPS = P // HEADS
BLOCKS = -(-EDGE_TILES // GROUPS)
ROW = BLOCKS * P
MID = -(-BLOCKS // 4)

BANKS = 4
D0_BANKS = (0, 1, 6, 7)
AHEAD = 4
VB, VSLOTS = 4, 4
VRING = VB * VSLOTS
UNROLL = 2 * VRING
MBATCH = EDGE_TILES // VB
XB = 3
XBATCH = EXTRA // XB
TILES = 4
BATCHES = -(-NODE_TILES // TILES)
PARTS = [(a, min(a + 13, NODE_TILES)) for a in range(0, NODE_TILES, 13)]
H_PARTS = 2

NO_NODE = 1 << 20
LOWEST = -3.0e38
ACCW = F + HEADS + 1

F32 = mybir.dt.float32
I32 = mybir.dt.int32
ALU = mybir.AluOpType
ACT = mybir.ActivationFunctionType
AX = mybir.AxisListType


def at_least(eng, sem, value):
    if isinstance(value, int) and value <= 0:
        return
    eng.wait_ge(sem, value)


def staged(eng, count, unroll, stages, setups=None, group=0):
    setups = setups or {}
    group = group or unroll
    most = max(lead for lead, _ in stages)
    rounds = (count - most) // unroll

    def peeled(first, end):
        values = {lead: [] for lead in setups}
        for i in range(first, end):
            for lead, f in setups.items():
                if 0 <= i + lead < count and not values[lead]:
                    values[lead] = list(f(i + lead, min(group, end - i, count - i - lead)))
            now = {lead: values[lead].pop(0) for lead in setups if 0 <= i + lead < count}
            for lead, body in stages:
                s = i + lead
                if 0 <= s < count:
                    body(s, s % unroll, s // unroll, *([now[lead]] if lead in setups else []))

    peeled(-most, unroll if rounds > 1 else count)
    if rounds > 1:
        with eng.Fori(1, rounds) as r:
            values = {lead: f(r * unroll + lead, unroll) for lead, f in setups.items()}
            for j in range(unroll):
                for lead, body in stages:
                    body(r * unroll + (j + lead), (j + lead) % unroll, r + (j + lead) // unroll,
                         *([values[lead][j]] if lead in setups else []))
        peeled(rounds * unroll, count)


def tile_batches(eng, stages):
    full = NODE_TILES // TILES
    staged(eng, full, 2, [(lead, lambda b, k, r, body=body: body(b, k, r, TILES)) for lead, body in stages])
    for _, body in sorted(stages, key=lambda stage: -stage[0]):
        body(full, full % 2, full // 2, NODE_TILES - full * TILES)


def reuse(eng, sem, s, depth, base=0):
    if isinstance(s, int) and s < depth:
        at_least(eng, sem, base)
    else:
        at_least(eng, sem, s + (base - depth + 1))


def slot_free(eng, sem, r):
    if isinstance(r, int) and r == 0:
        return
    eng.wait_ge(sem, 16 * r)


def graph_layers(nc, x, src, dst, rel, weight1, Wq, Wk, Wv, Wscale, W1, b1, W2, gate2, W3, out):
    ctx = ExitStack()
    with ctx:
        def sb(name, shape, dt=F32):
            return ctx.enter_context(nc.sbuf_tensor(name, shape, dt))

        def sem(name):
            return ctx.enter_context(nc.semaphore(name))

        def sems(name, n):
            return [sem(f"{name}{i}") for i in range(n)]

        def dram(name, shape, dt=F32):
            return nc.dram_tensor(name, shape, dt).ap()

        win_d = dram("win_d", (EDGE_TILES + 1,), I32)
        tile_d = dram("tile_d", (2, EXTRA), I32)
        rows_d = dram("rows_d", (EDGE_TILES, 4 * P))
        dst_d = dram("dst_d", (GROUPS * ROW + 2,), I32)
        qv_d = dram("qv_d", (NPAD, 2 * F))
        v_d = dram("v_d", (P, EDGE_TILES, F))
        t1_d = dram("t1_d", (NPAD, F + 1))
        t2_d = dram("t2_d", (NPAD * RELS, F))
        t3_d = dram("t3_d", (NPAD * RELS, F))

        X = sb("X", [P, NODE_TILES, F])
        H = sb("H", [P, NODE_TILES, F])
        SUMS = sb("SUMS", [P, NODE_TILES, ACCW])
        big = sb("big", [P, 2 * ROW])
        rows = sb("rows", [P, NODE_TILES * ACCW])
        col = sb("col", [P, 4, STEPS])
        SW = sb("SW", [P, STEPS, HEADS + 1])
        ring = sb("ring", [P, RING, 2 * F])
        idx = sb("idx", [P, RING], I32)
        onehot = sb("onehot", [P, RING, P])
        onehotT = sb("onehotT", [P, BANKS, P])
        prod = sb("prod", [P, 2, F])
        hs = sb("hs", [P, TILES, F])
        hT = sb("hT", [P, TILES, F])
        wraw = sb("wraw", [P, 4, F])
        wsraw = sb("wsraw", [P, HEADS, F])
        wqkvT = sb("wqkvT", [P, 3 * F])
        wsT = sb("wsT", [P, F])
        w1T = sb("w1T", [P, F])
        w2 = sb("w2", [P, RELS, F])
        w3 = sb("w3", [P, RELS, F])
        g2 = sb("g2", [P, RELS])
        bias = sb("bias", [P, F])
        iota_row = sb("iota_row", [P, P])
        iota_col = sb("iota_col", [P, 1])
        next_row = sb("next_row", [P, EXTRA])
        next_col = sb("next_col", [P, 1])
        ident = sb("ident", [P, P])
        one = sb("one", [1, 2])
        win = sb("win", [1, EDGE_TILES], I32)
        keep_at = sb("keep_at", [1, EDGE_TILES], I32)
        tile = sb("tile", [1, 2, EXTRA], I32)
        ends = sb("ends", [P, CHUNKS], I32)
        few = sb("few", [P, 8], I32)
        fewf = sb("fewf", [P, 8])
        stats = sb("stats", [P, NODE_TILES, 6])
        ln = sb("ln", [P, 4, NODE_TILES])
        rstd = sb("rstd", [P, NODE_TILES])
        shift = sb("shift", [P, NODE_TILES])
        rden = sb("rden", [P, NODE_TILES, HEADS])
        dinv = sb("dinv", [P, NODE_TILES])
        dtmp = sb("dtmp", [P, 2, NODE_TILES])
        carry = sb("carry", [P, 4])
        crow = sb("crow", [1, 4, P + 1])
        gate = sb("gate", [P, TILES, 2, RELS])
        minus1 = sb("minus1", [1, 4], I32)

        K = big[:, 0:NODE_TILES * F].rearrange("p (t f) -> p t f", f=F)
        ST = big[:, 0:ROW]
        FT = big[:, ROW:2 * ROW]
        RI = rows[:, 0:CHUNKS * 3 * P].bitcast(I32).rearrange("p (c k i) -> p c k i", c=CHUNKS, k=3)
        R = big[:, 0:CHUNKS * 4 * P].rearrange("p (c k i) -> p c k i", c=CHUNKS, k=4)
        spare = rows[:, CHUNKS * 3 * P:CHUNKS * 3 * P + 3 * (EDGE_TILES + 1)].rearrange("p (k e) -> p k e", k=3)
        keep_q = SUMS[:].rearrange("p t f -> p (t f)")[:, 0:NODE_TILES * F].rearrange("p (t f) -> p t f", f=F)
        keep_g = rows[:, 0:NODE_TILES * (F + 1)].rearrange("p (t f) -> p t f", f=F + 1)
        winb_i = spare[:, 0, :].bitcast(I32)
        winb = spare[:, 1, :]
        below = spare[:, 2, :]
        Tst = rows[:, 0:NODE_TILES * (F + 1)].rearrange("p (t f) -> p t f", f=F + 1)
        drow = rows[:, 0:ROW + 2].bitcast(I32)
        MT = rows[:, 0:ROW]
        pen = rows[:, ROW + 2:2 * ROW + 3]
        onehot_x0 = H[:]
        onehot_x = big[:, 0:EXTRA * P].rearrange("p (n i) -> p n i", i=P)
        hs8 = onehot[:].rearrange("p (k t) f -> p k t f", k=2)
        hT8 = ring[:, 0:4, :].rearrange("p (k a) (b f) -> p k (a b) f", k=2, b=2)
        y8 = ring[:, 4:8, :].rearrange("p (k a) (b f) -> p k (a b) f", k=2, b=2)
        hb8 = big[:, 0:2 * TILES * F].rearrange("p (k t f) -> p k t f", k=2, t=TILES)
        xrows = onehot[:].rearrange("p r f -> p (r f)")[:, 0:4 * P]
        vw = big[:, 0:VRING * ACCW].rearrange("p (r f) -> p r f", f=ACCW)
        odd_sums = rows[:].rearrange("p (t f) -> p t f", f=ACCW)
        onehot_v = big[:, VRING * ACCW:VRING * (ACCW + P)].rearrange("p (r f) -> p r f", f=P)
        vin = ring[:].rearrange("p r (two f) -> p (r two) f", two=2)
        qv_out = rows[:, ROW + 2:ROW + 2 + TILES * 2 * F].rearrange("p (k f) -> p k f", k=TILES)
        rel_out = rows[:, 0:TILES * RELS * F].rearrange("p (k f) -> p k f", k=TILES)

        ps = [ctx.enter_context(nc.psum_tensor(f"ps{i}", [P, 512], F32)) for i in range(8)]

        s_const = sem("s_const")
        s_edges = sem("s_edges")
        s_x = sem("s_x")
        s_w = sem("s_w")
        s_scratch = sem("s_scratch")
        s_extra = sem("s_extra")
        dve_step = sem("dve_step")
        act_step = sem("act_step")
        ROOTS = (1, 4, 5, 6)
        pe_prep = sem("pe_prep")
        s_dst = sem("s_dst")
        s_h1 = sem("s_h1")
        s_h1v = sem("s_h1v")
        s_t1d = sem("s_t1d")
        s_final = sem("s_final")
        s_out = sem("s_out")
        s_issued = sem("s_issued")
        s_mid_pe = sem("s_mid_pe")
        s_mid_cp = sem("s_mid_cp")
        s_fold = sem("s_fold")
        s_kept = sem("s_kept")
        s_weights = sem("s_weights")
        s_spread = sem("s_spread")
        s_zeroed = sem("s_zeroed")
        s_t1 = sem("s_t1")
        s_extra_hot = sem("s_extra_hot")

        q0 = dict(idx=sem("q0_idx"), rows=sems("q0_rows", RING), onehot=sem("q0_onehot"), turned=sem("q0_turned"),
                  copied=sem("q0_copied"), kexp=sem("q0_kexp"), prod=sem("q0_prod"), score=sem("q0_score"),
                  saved=sems("q0_saved", RING))
        a0 = dict(loaded=sems("a0_loaded", VSLOTS), vw=sem("a0_vw"), wcol=sem("a0_wcol"), onehot=sem("a0_onehot"),
                  distance=sem("a0_distance"), onehot_act=sem("a0_onehot_act"), summed=sem("a0_summed"),
                  added=sem("a0_added"))

        def gsems(name):
            return dict(idx=sem(name + "_idx"), rows=sems(name + "_rows", RING), onehot=sem(name + "_onehot"),
                        summed=sem(name + "_summed"), added=sem(name + "_added"), kept=sem(name + "_kept"))

        g1, gr2, gr3 = gsems("g1"), gsems("g2"), gsems("g3")

        def dsems(name, *more):
            s = {k: sem(f"{name}_{k}") for k in more}
            if name[0] == "d":
                s["stored"] = sems(name + "_stored", TILES)
            return s

        ln0 = dsems("ln0", "stats")
        d0 = dsems("d0", "h", "xadd", "turned", "hT", "prod", "qv", "k")
        p0 = dsems("p0", "inn", "turned", "T", "prod", "x", "stats")
        p1 = dsems("p1", "inn", "turned", "T", "prod", "hb", "hbd", "y", "yd", "z", "x", "stats")
        d2 = dsems("d2", "h", "turned", "hT", "gate", "gexp", "gone", "gsig", "prod", "dve", "act")
        p2 = dsems("p2", "x", "stats")
        d3 = dsems("d3", "h", "xadd", "turned", "hT", "prod", "dve", "act")

        block = ctx.enter_context(nc.Block())

        mark = {}

        def batch_free(eng, b, extra):
            if not extra:
                at_least(eng, a0["summed"], (b + 1) * VB - VRING)
            elif isinstance(b, int) and b < VSLOTS:
                eng.wait_ge(a0["summed"], EDGE_TILES)
            else:
                eng.wait_ge(a0["summed"], b * XB + (EDGE_TILES + XB - XB * VSLOTS))

        def table_waits(d):
            return [(d["stored"][k], 16 * len(range(k, NODE_TILES, TILES))) for k in range(TILES)]

        @block.vector
        def _(v):
            count = [0]

            def link(ins, name=None):
                count[0] += 1
                ins.then_inc(dve_step, 1)
                v.wait_ge(dve_step, count[0])
                if name:
                    mark[name] = count[0]

            win_regs = [v.alloc_register(f"win{k}") for k in range(UNROLL)]
            tile_regs = [v.alloc_register(f"tile{k}") for k in range(2 * RING)]

            def windows(s, n):
                v.reg_load(win_regs[0:n], win[0:1, bass.ds(s, n)])
                return [v.snap(r, min_val=0, max_val=NODE_TILES - 1) for r in win_regs[0:n]]

            def edge_tiles(s, n):
                v.reg_load(tile_regs[0:n], tile[0:1, 0, bass.ds(s, n)])
                return [v.snap(r, min_val=0, max_val=EDGE_TILES - 1) for r in tile_regs[0:n]]

            def kept(s, n):
                v.reg_load(win_regs[0:n], tile[0:1, 1, bass.ds(s, n)])
                return [v.snap(r, min_val=0, max_val=NODE_TILES - 1) for r in win_regs[0:n]]

            v.wait_ge(s_const, 2)
            link(v.tensor_scalar(ident[:], iota_row[:], iota_col[:, 0:1], None, ALU.is_equal), "ident")
            v.wait_ge(s_edges, 12 * 16)
            link(v.tensor_scalar(ends[:], RI[:, :, 0, P - 1], 7, None, ALU.arith_shift_right))
            link(v.tensor_scalar(ends[:], ends[:], float(NODE_TILES - 1), None, ALU.min), "ends")
            link(v.tensor_copy(R[:, :, 0:2, :], RI[:, :, 0:2, :]))
            link(v.scalar_tensor_tensor(R[:, :, 2, :], RI[:, :, 1, :], float(RELS), RI[:, :, 2, :],
                                        ALU.mult, ALU.add), "rows")
            v.wait_ge(s_x, 32)
            staged(v, NODE_TILES, 4 * TILES, [(0, lambda s, k, r: v.bn_stats(
                stats[:, bass.ds(s, 1), :], X[:, bass.ds(s, 1), :]).then_inc(ln0["stats"], 1))])
            v.wait_ge(s_scratch, 16 * 7)
            link(v.tensor_copy(winb[:], winb_i[:]))
            link(v.tensor_scalar(below[0:EXTRA, 0:EDGE_TILES], winb[0:EXTRA, 1:EDGE_TILES + 1],
                                 next_col[0:EXTRA, 0:1], None, ALU.is_lt))
            link(v.tensor_reduce(fewf[0:EXTRA, 0:1], below[0:EXTRA, 0:EDGE_TILES], AX.X, ALU.add))
            link(v.scalar_tensor_tensor(below[0:EXTRA, 0:EDGE_TILES], below[0:EXTRA, 0:EDGE_TILES], float(P),
                                        winb[0:EXTRA, 1:EDGE_TILES + 1], ALU.mult, ALU.add))
            link(v.tensor_reduce(fewf[0:EXTRA, 1:2], below[0:EXTRA, 0:EDGE_TILES], AX.X, ALU.min))
            link(v.tensor_copy(few[0:EXTRA, 0:2], fewf[0:EXTRA, 0:2]), "tiles")
            link(v.tensor_tensor(below[0:1, 0:EDGE_TILES], winb[0:1, 1:EDGE_TILES + 1], winb[0:1, 0:EDGE_TILES], ALU.is_gt))
            link(v.tensor_tensor(keep_at[:], below[0:1, 0:EDGE_TILES], winb[0:1, 1:EDGE_TILES + 1], ALU.mult), "keep_at")
            for c in range(CHUNKS + 1):
                w = P if c < CHUNKS - 1 else CTAIL if c == CHUNKS - 1 else EXTRA
                v.wait_ge(pe_prep, c + 1)
                o = c * P if c < CHUNKS else EDGE_TILES
                link(v.tensor_copy(col[:, :, o:o + w],
                                   ps[c][:].rearrange("p (k i) -> p k i", k=4)[:, :, 0:w]), f"col{c}")
            link(v.scalar_tensor_tensor(col[:, 0, 0:EDGE_TILES], winb[:, 0:EDGE_TILES], -float(P), col[:, 0, 0:EDGE_TILES],
                                        ALU.mult, ALU.add))
            link(v.scalar_tensor_tensor(col[:, 0, EDGE_TILES:STEPS], next_row[:], -float(P),
                                        col[:, 0, EDGE_TILES:STEPS], ALU.mult, ALU.add), "cols")
            v.wait_ge(s_w, 16 * 9)
            link(v.tensor_reduce(hs[:, 0, :], wsraw[:].rearrange("p h c -> p c h"), AX.X, ALU.add), "wsum")
            v.wait_ge(pe_prep, CHUNKS + 2)
            link(v.tensor_scalar(wqkvT[:, 0:F], ps[0][:, 0:F], HDIM ** -0.5, None, ALU.mult))
            link(v.tensor_copy(wqkvT[:, F:2 * F], ps[0][:, 2 * F:3 * F]))
            link(v.tensor_copy(wqkvT[:, 2 * F:3 * F], ps[0][:, F:2 * F]))
            link(v.tensor_copy(w1T[:], ps[0][:, 3 * F:4 * F]))
            link(v.tensor_copy(wsT[:], ps[1][:, 0:F]), "weights")

            def norm_stats(done):
                me, qe, mo, qo = (stats[:, :, j] for j in (1, 2, 4, 5))
                v.wait_ge(done, NODE_TILES)
                link(v.tensor_tensor(ln[:, 0, :], me, mo, ALU.add))
                link(v.tensor_tensor(ln[:, 1, :], me, mo, ALU.subtract))
                link(v.tensor_tensor(ln[:, 2, :], qe, qo, ALU.add))
                link(v.tensor_tensor(ln[:, 1, :], ln[:, 1, :], ln[:, 1, :], ALU.mult))
                link(v.tensor_scalar(ln[:, 2, :], ln[:, 2, :], 1.0 / F, EPS, ALU.mult, ALU.add))
                link(v.scalar_tensor_tensor(ln[:, 3, :], ln[:, 1, :], 0.25, ln[:, 2, :], ALU.mult, ALU.add),
                     f"var{len([m for m in mark if m.startswith('var')])}")

            def norm_scale(n):
                v.wait_ge(act_step, ROOTS[n])
                link(v.reciprocal(rstd[:], ln[:, 3, :]))
                link(v.scalar_tensor_tensor(shift[:], ln[:, 0, :], -0.5, rstd[:], ALU.mult, ALU.mult), f"ln{n}")

            norm_stats(ln0["stats"])
            norm_scale(0)

            def hT_copy(d, banks=(0, 1)):
                def body(s, k, r):
                    v.wait_ge(d["turned"], s + 1)
                    at_least(v, d["prod"], s - TILES + 1)
                    v.tensor_copy(hT[:, k, :], ps[banks[k % len(banks)]][:, 0:F]).then_inc(d["hT"], 1)
                return body

            def one_hot(where, step, weighted):
                return v.tensor_scalar(where, iota_row[:], col[:, 0, bass.ds(step, 1)],
                                       col[:, 3, bass.ds(step, 1)] if weighted else None, ALU.is_equal,
                                       **({"op1": ALU.mult} if weighted else {}))

            def build_extra(where, weighted=False):
                def body(s, k, r):
                    if not (isinstance(s, int) and s >= EXTRA):
                        one_hot(where[:, bass.ds(s, 1), :].rearrange("p a i -> p (a i)"), s + EDGE_TILES,
                                weighted).then_inc(s_extra_hot, 1)
                return body

            def d0_k(s, k, r):
                v.wait_ge(d0["prod"], s + 1)
                v.tensor_copy(K[:, bass.ds(s, 1), :],
                              ps[4 + k % 2][:, 0:F].rearrange("p (a f) -> p a f", a=1)).then_inc(d0["k"], 1)

            staged(v, NODE_TILES, TILES, [(2, hT_copy(d0, D0_BANKS)), (0, d0_k), (0, build_extra(onehot_x0))])

            def build(s, k, done, sig, weighted=False):
                at_least(v, done, s - RING + 1)
                one_hot(onehot[:, k, :], s, weighted).then_inc(sig, 1)

            v.wait_ge(d0["k"], NODE_TILES)

            def scores(count, base, rows_of, more_stages, setups):
                first = len(more_stages)

                def make(s, k, r):
                    build(s, k, q0["turned"], q0["onehot"])

                def times(s, k, r, *at):
                    v.wait_ge(q0["kexp"], s + (base + 1))
                    reuse(v, q0["score"], s, 2, base)
                    v.tensor_tensor(prod[:, k % 2, :], rows_of(k, r, *at), ps[4 + k % BANKS][:, 0:F],
                                    ALU.mult).then_inc(q0["prod"], 1)

                def total(s, k, r):
                    v.wait_ge(q0["prod"], s + (base + 1))
                    v.tensor_reduce(SW[:, bass.ds(s + base, 1), 0:HEADS],
                                    prod[:, k % 2, :].rearrange("p (a h d) -> p a h d", a=1, h=HEADS),
                                    AX.X, ALU.add).then_inc(q0["score"], 1)

                staged(v, count, 2 * RING if base else RING, [(AHEAD + 1, make)] * (not base) + [(first + 1, times), (first, total)]
                       + more_stages, setups)

            def gathered(k, r):
                v.wait_ge(q0["rows"][k], 16 * (r + 1))
                return ring[:, k, 0:F]

            def kept_row(k, r, at):
                return keep_q[:, bass.ds(at, 1), :].rearrange("p a f -> p (a f)")

            def fold(s, k, r, e):
                v.wait_ge(q0["score"], s + (EDGE_TILES + 1))
                at_least(v, s_fold, s)
                v.tensor_tensor(SW[:, bass.ds(e, 1), 0:HEADS], SW[:, bass.ds(e, 1), 0:HEADS],
                                SW[:, bass.ds(s + EDGE_TILES, 1), 0:HEADS], ALU.add).then_inc(s_fold, 1)

            for d, n in table_waits(d0):
                v.wait_ge(d, n)
            v.wait_ge(s_dst, 128)
            link(v.tensor_tensor(pen[:], drow[:, 1:ROW + 2], drow[:, 0:ROW + 1], ALU.not_equal))
            link(v.tensor_scalar(pen[:], pen[:], LOWEST, None, ALU.mult))
            scores(EDGE_TILES, 0, gathered, [], {})
            v.wait_ge(s_scratch, 16 * 10)
            v.wait_ge(s_kept, EDGE_TILES)
            scores(EXTRA, EDGE_TILES, kept_row, [(0, fold)], {2: kept, 0: edge_tiles})

            SWt = SW[:, 0:GROUPS * BLOCKS, 0:HEADS].rearrange("p (g b) h -> p b h g", b=BLOCKS)
            v.wait_ge(s_fold, EXTRA)
            link(v.tensor_copy(FT.rearrange("p (b h g) -> p b h g", b=BLOCKS, h=HEADS), SWt), "blocks")
            for b in range(0, BLOCKS, 4):
                n = min(4, BLOCKS - b)
                v.wait_ge(s_mid_pe, b // 4 + 1)
                v.tensor_copy(ST[:, b * P:(b + n) * P], ps[(b // 4) % 2][:, 0:n * P]).then_inc(s_mid_cp, 1)
            v.wait_ge(s_mid_cp, MID)
            link(v.tensor_tensor_scan(FT, pen[:, 0:ROW], ST, LOWEST, ALU.add, ALU.max))
            link(v.tensor_tensor(carry[:, 0:1], drow[:, ROW:ROW + 1], drow[:, 0:1], ALU.not_equal))
            link(v.tensor_scalar(carry[:, 1:2], carry[:, 0:1], LOWEST, None, ALU.mult))
            link(v.tensor_copy(carry[:, 0:1], FT[:, ROW - 1:ROW]), "carry_f")
            v.wait_ge(s_mid_pe, MID + 1)
            link(v.tensor_copy(crow[:, 0:2, 1:P + 1], ps[2][0:1, 0:2 * P].rearrange("p (k i) -> p k i", k=2)))
            link(v.tensor_tensor_scan(crow[:, 2, 1:P + 1], crow[:, 1, 1:P + 1], crow[:, 0, 1:P + 1],
                                      LOWEST, ALU.add, ALU.max))
            link(v.memset(crow[:, 2, 0:1], LOWEST), "crow_f")
            v.wait_ge(s_mid_pe, MID + 2)
            link(v.tensor_copy(carry[:, 2:3], ps[3][:, 0:1]))
            link(v.tensor_tensor_scan(FT, pen[:, 0:ROW], ST, carry[:, 2:3], ALU.add, ALU.max))
            link(v.tensor_tensor(carry[:, 0:1], drow[:, 1:2], drow[:, ROW + 1:ROW + 2], ALU.not_equal))
            link(v.tensor_scalar(carry[:, 1:2], carry[:, 0:1], LOWEST, None, ALU.mult))
            link(v.tensor_tensor_scan(MT[:, ::-1], pen[:, 1:ROW + 1][:, ::-1], FT[:, ::-1], LOWEST, ALU.add, ALU.max))
            link(v.tensor_copy(carry[:, 0:1], MT[:, 0:1]), "carry_b")
            v.wait_ge(s_mid_pe, MID + 3)
            link(v.tensor_copy(crow[:, 0:2, 0:P], ps[4][0:1, 0:2 * P].rearrange("p (k i) -> p k i", k=2)))
            link(v.tensor_tensor_scan(crow[:, 2, 0:P][:, ::-1], crow[:, 1, 0:P][:, ::-1], crow[:, 0, 0:P][:, ::-1],
                                      LOWEST, ALU.add, ALU.max))
            link(v.memset(crow[:, 2, P:P + 1], LOWEST), "crow_b")
            v.wait_ge(s_mid_pe, MID + 4)
            link(v.tensor_copy(carry[:, 3:4], ps[5][:, 0:1]))
            link(v.tensor_tensor_scan(MT[:, ::-1], pen[:, 1:ROW + 1][:, ::-1], FT[:, ::-1], carry[:, 3:4], ALU.add, ALU.max))
            link(v.tensor_tensor(FT, ST, MT, ALU.subtract), "diff")
            for b in range(0, BLOCKS, 4):
                n = min(4, BLOCKS - b)
                v.wait_ge(s_mid_pe, MID + 4 + b // 4 + 1)
                v.tensor_copy(SWt[:, b:b + n], ps[(b // 4) % 4][:, 0:n * P].rearrange("p (b h g) -> p b h g", b=n, h=HEADS)).then_inc(s_mid_cp, 1)
            v.wait_ge(s_mid_cp, 2 * MID)
            v.sem_inc(s_weights, 1)

            def add(width, g, sums, chains):
                def body(s, k, r, w):
                    at = bass.ds(w, 1)
                    v.wait_ge(g["summed"], s + 1)
                    at_least(v, g["added"], s - chains + 1)
                    to = sums[k % chains]
                    v.tensor_tensor(to[:, at, 0:width], to[:, at, 0:width],
                                    ps[k % RING][:, 0:width].rearrange("p (a f) -> p a f", a=1), ALU.add).then_inc(g["added"], 1)
                return body

            def add_extra(width, g, after=()):
                def body(b, k, r):
                    v.wait_ge(g["summed"], b * XB + (EDGE_TILES + XB))
                    to = SUMS[:, bass.ds(b * XB + 1, XB), 0:width]
                    v.tensor_tensor(to, to, ps[k][:, 0:XB * width].rearrange("p (a f) -> p a f", a=XB), ALU.add).then_inc(g["added"], 1)

                def follow(stage):
                    return lambda b, k, r: stage(b * XB + 1, XB, b + 2)

                for stage in after:
                    stage(0, 1, 1)
                staged(v, XBATCH, VSLOTS, [(len(after), body)]
                       + [(len(after) - 1 - i, follow(stage)) for i, stage in enumerate(after)])
                v.wait_ge(g["added"], EDGE_TILES + XBATCH)

            def sum_pass(g, n, width, weighted, after=()):
                v.wait_ge(s_zeroed, n)
                staged(v, EDGE_TILES, RING, [(AHEAD, lambda s, k, r: build(s, k, g["summed"], g["onehot"], weighted)),
                                             (0, add(width, g, [SUMS], 1))], {0: windows})
                v.wait_ge(g["added"], EDGE_TILES)
                add_extra(width, g, after)

            def make_pair(s, k, r):
                if k % VB == 0:
                    at_least(v, a0["summed"], s + (2 - VRING))
                    at = k % VRING
                    v.tensor_tensor(onehot_v[:, at:at + 2, :], iota_row[:].unsqueeze(1).to_broadcast([P, 2, P]),
                                    col[:, 0, bass.ds(s, 2)].unsqueeze(2).to_broadcast([P, 2, P]),
                                    ALU.is_equal).then_inc(a0["onehot"], 1)

            v.wait_ge(s_zeroed, 1)
            staged(v, EDGE_TILES, UNROLL, [(0, add(ACCW, a0, [SUMS, odd_sums], 2)), (2 * VB + 1, make_pair)], {0: windows})
            v.wait_ge(a0["added"], EDGE_TILES)
            link(v.tensor_tensor(SUMS[:], SUMS[:], odd_sums, ALU.add))
            add_extra(ACCW, a0)
            SUMh = SUMS[:, :, 0:F]
            den = SUMS[:, :, F:F + HEADS]
            deg = SUMS[:, :, F + HEADS]
            link(v.scalar_tensor_tensor(rden[:], den, 0.0, den, ALU.is_equal, ALU.add))
            link(v.reciprocal(rden[:], rden[:]))
            link(v.scalar_tensor_tensor(dtmp[:, 0, :], deg, 0.0, deg, ALU.is_equal, ALU.add), "deg")

            def node_add(p, source):
                def body(b, k, r, n):
                    v.wait_ge(p["prod" if source is None else "z"], b + 1)
                    at = X[:, bass.ds(b * TILES, n), :]
                    v.tensor_tensor(at, at, source[:, k, 0:n, :] if source is not None else
                                    ps[4 + k][:, 0:n * F].rearrange("p (t f) -> p t f", t=n), ALU.add).then_inc(p["x"], 1)
                return body

            def batch_stats(p):
                def body(b, k, r, n):
                    v.wait_ge(p["x"], b + 1)
                    for i in range(n):
                        v.bn_stats(stats[:, bass.ds(b * TILES + i, 1), :], X[:, bass.ds(b * TILES + i, 1), :]).then_inc(p["stats"], 1)
                return body

            v.wait_ge(d0["xadd"], NODE_TILES)
            tile_batches(v, [(1, node_add(p0, None)), (0, batch_stats(p0))])
            norm_stats(p0["stats"])
            norm_scale(1)
            v.wait_ge(act_step, 3)
            link(v.reciprocal(dtmp[:, 1, :], dtmp[:, 0, :]))
            link(v.scalar_tensor_tensor(dinv[:], deg, 0.0, dtmp[:, 1, :], ALU.is_gt, ALU.mult), "dinv")

            first = PARTS[H_PARTS][0]

            def h1(s, k, r):
                at = bass.ds(s + first, 1)
                v.tensor_scalar(H[:, at, :], X[:, at, :], rstd[:, at], shift[:, at], ALU.mult, ALU.add).then_inc(s_h1v, 1)

            link(v.tensor_copy(Tst[:, :, F], dinv[:]))
            staged(v, NODE_TILES - first, RING, [(0, h1)])
            v.wait_ge(s_h1v, NODE_TILES - first)
            link(v.tensor_scalar(H[:, first:, :], H[:, first:, :], 0.0, None, ALU.max))
            for a, b in PARTS[H_PARTS:] + PARTS[:H_PARTS]:
                if b <= first:
                    v.wait_ge(s_h1, b)
                v.tensor_tensor(Tst[:, a:b, 0:F], H[:, a:b, :], dinv[:, a:b].unsqueeze(2).to_broadcast([P, b - a, F]),
                                ALU.mult).then_inc(s_t1, 1)
            sum_pass(g1, 2, F + 1, False)

            def p1_y(b, k, r, n):
                v.wait_ge(p1["prod"], b + 1)
                v.wait_ge(p1["hbd"], b + 1)
                at_least(v, p1["x"], b - 1)
                v.tensor_tensor(y8[:, k, 0:n, :], hb8[:, k, 0:n, :], ps[4 + k][:, 0:n * F].rearrange("p (t f) -> p t f", t=n),
                                ALU.add).then_inc(p1["y"], 1)

            def p1_z(b, k, r, n):
                v.wait_ge(p1["yd"], b + 1)
                at = y8[:, k, 0:n, :]
                v.scalar_tensor_tensor(at, at, SLOPE, at, ALU.mult, ALU.max).then_inc(p1["z"], 1)

            tile_batches(v, [(2, p1_y), (1, p1_z), (0, batch_stats(p1)), (1, node_add(p1, y8))])
            norm_stats(p1["stats"])
            norm_scale(2)

            half = RELS // 2 * F

            def d2_add(s, k, r):
                v.wait_ge(d2["gexp"], s + 1)
                v.tensor_scalar(gate[:, k, 1, :], gate[:, k, 0, :], 1.0, None, ALU.add).then_inc(d2["gone"], 1)

            def d2_gate(s, k, r):
                v.wait_ge(d2["gone"], s + 1)
                at_least(v, d2["act"], s - TILES + 1)
                v.reciprocal(gate[:, k, 0, :], gate[:, k, 1, :]).then_inc(d2["gsig"], 1)

            def d2_out(s, k, r):
                v.wait_ge(d2["gsig"], s + 1)
                v.wait_ge(d2["prod"], s + 1)
                slot_free(v, d2["stored"][k], r)
                v.tensor_tensor(rel_out[:, k, 0:half].rearrange("p (q f) -> p q f", f=F),
                                ps[4 + 2 * (k % 2)][:].rearrange("p (q f) -> p q f", f=F),
                                gate[:, k, 0, 0:RELS // 2].unsqueeze(2).to_broadcast([P, RELS // 2, F]),
                                ALU.mult).then_inc(d2["dve"], 1)

            staged(v, NODE_TILES, TILES, [(2, hT_copy(d2)), (1, d2_add), (1, d2_gate), (0, d2_out), (0, build_extra(onehot_x, True))])

            def p2_x(at, n, turn):
                v.wait_ge(gr2["added"], turn + (EDGE_TILES - 1))
                to = X[:, bass.ds(at, n), :]
                v.scalar_tensor_tensor(to, SUMS[:, bass.ds(at, n), 0:F], 0.0, to, ALU.max, ALU.add).then_inc(p2["x"], 1)

            def p2_stats(at, n, turn):
                v.wait_ge(p2["x"], turn)
                for i in range(n):
                    v.bn_stats(stats[:, bass.ds(at + i, 1), :], X[:, bass.ds(at + i, 1), :]).then_inc(p2["stats"], 1)

            sum_pass(gr2, 3, F, True, [p2_x, p2_stats])
            norm_stats(p2["stats"])
            norm_scale(3)

            def d3_out(s, k, r):
                v.wait_ge(d3["prod"], s + 1)
                slot_free(v, d3["stored"][k], r)
                v.tensor_copy(rel_out[:, k, 0:half], ps[4 + 2 * (k % 2)][:]).then_inc(d3["dve"], 1)

            staged(v, NODE_TILES, TILES, [(2, hT_copy(d3)), (0, d3_out), (0, build_extra(onehot_x))])

            def final(at, n, turn):
                v.wait_ge(gr3["added"], turn + (EDGE_TILES - 1))
                to = X[:, bass.ds(at, n), :]
                v.tensor_tensor(to, to, SUMS[:, bass.ds(at, n), 0:F], ALU.add).then_inc(s_final, 1)

            v.wait_ge(d3["xadd"], NODE_TILES)
            sum_pass(gr3, 4, F, False, [final])

        @block.gpsimd
        def _(g):
            g.memset(RI[:, :, 0, :], NO_NODE)
            g.memset(RI[:, :, 1:3, :], 0)
            g.memset(R[:, :, 3, :], 0.0)
            g.memset(X[:, NODE_TILES - 1, :], 0.0).then_inc(s_const, 1)
            g.iota(iota_row[:], [[1, P]], base=0, channel_multiplier=0, allow_small_or_imprecise_dtypes=True)
            g.iota(iota_col[:], [[0, 1]], base=0, channel_multiplier=1, allow_small_or_imprecise_dtypes=True)
            g.iota(next_row[:], [[1, EXTRA]], base=1, channel_multiplier=0, allow_small_or_imprecise_dtypes=True)
            g.iota(next_col[:], [[0, 1]], base=1, channel_multiplier=1, allow_small_or_imprecise_dtypes=True)
            g.memset(one[:], 1.0)
            g.memset(minus1[:, 0:1], -1)
            g.memset(minus1[:, 1:2], NO_NODE)
            g.memset(minus1[:, 2:3], 0)
            g.memset(SW[:], 1.0)
            g.memset(keep_q[:, 0, :], 0.0).then_inc(s_const, 1)

            g.wait_ge(dve_step, mark["tiles"])
            g.wait_ge(s_scratch, 16 * 5)
            g.indirect_dma_start(xrows[0:EXTRA, :], None, rows_d[:, :],
                                 bass.IndirectOffsetOnAxis(ap=few[0:EXTRA, 0:1], axis=0)).then_inc(s_extra, 16)

            def xadd(d, s, k):
                g.wait_ge(d["h"], s + 1)
                g.tensor_tensor(X[:, bass.ds(s, 1), :], X[:, bass.ds(s, 1), :],
                                hs[:, k, :].rearrange("p (a f) -> p a f", a=1), ALU.add).then_inc(d["xadd"], 1)

            staged(g, NODE_TILES, TILES, [(0, lambda s, k, r: xadd(d0, s, k))])

            def waited():
                g.sem_inc(s_issued, 1)

            def gather(q, table, width, freed, written):
                def body(s, k, r):
                    for name, free in freed:
                        if name == "step":
                            reuse(g, free, s, RING)
                        else:
                            slot_free(g, free[k], r)
                    for d, n in written:
                        g.wait_ge(d, n)
                    g.wait_ge(q["idx"], s + 1)
                    waited()
                    g.indirect_dma_start(ring[:, k, 0:width], None, table,
                                         bass.IndirectOffsetOnAxis(ap=idx[:, k:k + 1], axis=0)).then_inc(q["rows"][k], 16)
                staged(g, EDGE_TILES, RING, [(0, body)])

            table_done = table_waits(d0)
            gather(q0, qv_d[:, :], 2 * F, [("step", q0["prod"]), ("step", s_kept), ("slot", q0["saved"])], table_done)

            def zero(waits):
                for d, n in waits:
                    g.wait_ge(d, n)
                g.memset(SUMS[:], 0.0).then_inc(s_zeroed, 1)

            g.wait_ge(q0["score"], STEPS)
            g.memset(SUMS[:], 0.0)
            g.wait_ge(dve_step, mark["diff"])
            g.memset(odd_sums, 0.0).then_inc(s_zeroed, 1)

            g.wait_ge(s_weights, 1)

            def weigh(batch, n):
                extra = n == XB

                def body(b, j, r):
                    if extra:
                        g.wait_ge(a0["loaded"][j], 16 * (MBATCH // VSLOTS) + 16 * XB * (r + 1))
                    else:
                        g.wait_ge(a0["loaded"][j], 16 * (r + 1))
                    batch_free(g, b, extra)
                    g.tensor_tensor(vw[:, j * VB:j * VB + n, 0:F].rearrange("p s (h d) -> p s h d", h=HEADS),
                                    vin[:, j * VB:j * VB + n, :].rearrange("p s (h d) -> p s h d", h=HEADS),
                                    SW[:, bass.ds(b * n + EDGE_TILES * extra, n), 0:HEADS].unsqueeze(3).to_broadcast([P, n, HEADS, HDIM]),
                                    ALU.mult).then_inc(a0["vw"], 1)
                staged(g, batch, VSLOTS, [(0, body)])

            weigh(MBATCH, VB)
            g.wait_ge(s_spread, EXTRA)
            weigh(XBATCH, XB)

            def p0_in(b, k, r, n):
                at_least(g, p0["turned"], b - 1)
                waited()
                g.tensor_tensor(hs8[:, k, 0:n, :].rearrange("p t (h d) -> p t h d", h=HEADS),
                                SUMS[:, bass.ds(b * TILES, n), 0:F].rearrange("p t (h d) -> p t h d", h=HEADS),
                                rden[:, bass.ds(b * TILES, n), :].unsqueeze(3).to_broadcast([P, n, HEADS, HDIM]),
                                ALU.mult).then_inc(p0["inn"], 1)

            g.wait_ge(dve_step, mark["deg"])
            tile_batches(g, [(0, p0_in)])
            zero([(dve_step, mark["dinv"]), (p0["inn"], BATCHES)])

            gather(g1, t1_d[:, :], F + 1, [("step", g1["summed"]), ("step", g1["kept"])], [(s_t1d, 16 * len(PARTS))])

            def p1_in(b, k, r, n):
                at_least(g, p1["turned"], b - 1)
                waited()
                g.tensor_tensor(hs8[:, k, 0:n, :], SUMS[:, bass.ds(b * TILES, n), 0:F], H[:, bass.ds(b * TILES, n), :],
                                ALU.mult).then_inc(p1["inn"], 1)

            def add_bias(b, k, r, n):
                at_least(g, p1["y"], b - 1)
                waited()
                g.tensor_tensor(hb8[:, k, 0:n, :], H[:, bass.ds(b * TILES, n), :], bias[:].unsqueeze(1).to_broadcast([P, n, F]),
                                ALU.add).then_inc(p1["hb"], 1)

            g.wait_ge(g1["added"], EDGE_TILES + XBATCH)
            tile_batches(g, [(1, p1_in), (0, add_bias)])
            zero([(p1["hbd"], BATCHES), (p1["inn"], BATCHES)])
            table_done = table_waits(d2)
            gather(gr2, t2_d[:, :], F, [("step", gr2["summed"]), ("step", gr2["kept"])], table_done)
            zero([(p2["x"], XBATCH + 1)])
            staged(g, NODE_TILES, TILES, [(0, lambda s, k, r: xadd(d3, s, k))])
            table_done = table_waits(d3)
            gather(gr3, t3_d[:, :], F, [("step", gr3["summed"]), ("step", gr3["kept"])], table_done)

        @block.scalar
        def _(a):
            def root(n):
                a.wait_ge(dve_step, mark[f"var{n}"])
                a.activation(ln[:, 3, :], ln[:, 3, :], ACT.Sqrt).then_inc(act_step, 1)

            def normed(d):
                def body(s, k, r):
                    at_least(a, d["turned"], s - TILES + 1)
                    if "xadd" in d:
                        at_least(a, d["xadd"], s - TILES + 1)
                    a.activation(hs[:, k, :].rearrange("p (a f) -> p a f", a=1), X[:, bass.ds(s, 1), :], ACT.Relu,
                                 bias=shift[:, bass.ds(s, 1)], scale=rstd[:, bass.ds(s, 1)]).then_inc(d["h"], 1)
                return body

            root(0)
            a.wait_ge(dve_step, mark["ln0"])

            def d0_out(s, k, r):
                a.wait_ge(d0["prod"], s + 1)
                slot_free(a, d0["stored"][k], r)
                a.activation(qv_out[:, k, :], ps[2 + k % 2][:, 0:2 * F], ACT.Copy).then_inc(d0["qv"], 1)

            staged(a, NODE_TILES, TILES, [(3, normed(d0)), (0, d0_out)])

            def index(q, kind):
                def body(s, k, r):
                    slot_free(a, q["rows"][k], r)
                    a.activation(idx[:, k:k + 1], col[:, kind, bass.ds(s, 1)], ACT.Copy).then_inc(q["idx"], 1)
                return body

            a.wait_ge(dve_step, mark["cols"])

            def q0_copy(base):
                def body(s, k, r):
                    a.wait_ge(q0["turned"], s + (base + 1))
                    reuse(a, q0["kexp"], s, BANKS, base)
                    a.activation(onehotT[:, k % BANKS, :], ps[k % BANKS][:, 0:P], ACT.Copy).then_inc(q0["copied"], 1)
                return body

            keep_regs = [a.alloc_register(f"keep{k}") for k in range(RING)]

            def keep_slots(s, n):
                a.reg_load(keep_regs[0:n], keep_at[0:1, bass.ds(s, n)])
                return [a.snap(r, min_val=0, max_val=NODE_TILES - 1) for r in keep_regs[0:n]]

            def keep(q, where, width, done):
                def body(s, k, r, at):
                    a.wait_ge(q["rows"][k], 16 * (r + 1))
                    at_least(a, done, s)
                    a.activation(where[:, bass.ds(at, 1), 0:width], ring[:, k, 0:width].rearrange("p (a f) -> p a f", a=1),
                                 ACT.Copy).then_inc(done, 1)
                return body

            staged(a, EDGE_TILES, RING, [(2, q0_copy(0)), (0, keep(q0, keep_q, F, s_kept)), (RING, index(q0, 1))],
                   {0: keep_slots})
            staged(a, EXTRA, RING, [(0, q0_copy(EDGE_TILES))])

            a.wait_ge(dve_step, mark["diff"])
            a.activation(ST, FT, ACT.Exp).then_inc(act_step, 1)

            a.wait_ge(s_weights, 1)

            def wcol(first, batch, n, more_stages=(), setups=None):
                extra = n == XB

                def columns(b, j, r, *_):
                    j = j % VSLOTS
                    batch_free(a, b + first, extra)
                    a.activation(vw[:, j * VB:j * VB + n, F:ACCW], SW[:, bass.ds(b * n + (first * n + EDGE_TILES * extra), n), :],
                                 ACT.Copy).then_inc(a0["wcol"], 1)

                def distance(b, j, r, *_):
                    o = j % VSLOTS * VB
                    for i in (2, 3):
                        a.activation(onehot_v[:, o + i, :], iota_row[:], ACT.Abs, scale=-1.0,
                                     bias=col[:, 0, bass.ds(b * VB + (first * VB + i), 1)]).then_inc(a0["distance"], 1)

                def near(b, j, r, *_):
                    o = j % VSLOTS * VB
                    a.wait_ge(a0["distance"], b * 2 + (first * 2 + 2))
                    a.activation(onehot_v[:, o + 2:o + 4, :], onehot_v[:, o + 2:o + 4, :], ACT.Relu, scale=-1.0,
                                 bias=SW[:, 0, HEADS:HEADS + 1]).then_inc(a0["onehot_act"], 1)

                stages = [(0, columns)] if extra else [(1, columns), (1, distance), (0, near)]
                staged(a, batch, 2 * VSLOTS if more_stages else VSLOTS, stages + list(more_stages), setups)

            def edge_tiles(s, n):
                a.reg_load(keep_regs[0:n], tile[0:1, 0, bass.ds(s, n)])
                return [a.snap(r, min_val=0, max_val=EDGE_TILES - 1) for r in keep_regs[0:n]]

            def spread(s, k, r, e):
                a.activation(SW[:, bass.ds(s + EDGE_TILES, 1), :], SW[:, bass.ds(e, 1), :], ACT.Copy).then_inc(s_spread, 1)

            wcol(0, EXTRA, VB, [(0, spread)], {0: edge_tiles})
            wcol(EXTRA, MBATCH - EXTRA, VB)
            a.wait_ge(s_spread, EXTRA)
            wcol(0, XBATCH, XB)
            a.wait_ge(a0["summed"], STEPS)
            a.activation(onehot_x, onehot_x0[:, 0:EXTRA, :], ACT.Copy).then_inc(s_extra_hot, 1)
            a.wait_ge(dve_step, mark["deg"])
            a.activation(dtmp[:, 0, :], dtmp[:, 0, :], ACT.Sqrt).then_inc(act_step, 1)

            def pass_rows(q, kind, width):
                staged(a, EDGE_TILES, RING, [(0, keep(q, keep_g, width, q["kept"])), (RING, index(q, kind))],
                       {0: keep_slots})

            def turned_copy(p):
                def body(b, k, r, n):
                    a.wait_ge(p["turned"], b + 1)
                    at_least(a, p["prod"], b - 1)
                    a.activation(hT8[:, k, 0:n, :], ps[k][:, 0:n * F].rearrange("p (t f) -> p t f", t=n), ACT.Copy).then_inc(p["T"], 1)
                return body

            tile_batches(a, [(0, turned_copy(p0))])
            root(1)
            a.wait_ge(dve_step, mark["ln1"])
            staged(a, PARTS[H_PARTS][0], RING, [(0, lambda s, k, r: a.activation(
                H[:, bass.ds(s, 1), :], X[:, bass.ds(s, 1), :], ACT.Relu,
                bias=shift[:, bass.ds(s, 1)], scale=rstd[:, bass.ds(s, 1)]).then_inc(s_h1, 1))])

            pass_rows(g1, 1, F + 1)

            def scaled(rows8, wait, done, scale):
                def body(b, k, r, n):
                    a.wait_ge(p1[wait], b + 1)
                    for i in range(n):
                        ins = a.activation(rows8[:, k, i, :], rows8[:, k, i, :], ACT.Copy, scale=scale(b * TILES + i))
                    ins.then_inc(p1[done], 1)
                return body

            tile_batches(a, [(1, scaled(hb8, "hb", "hbd", lambda t: SUMS[:, bass.ds(t, 1), F:F + 1].rearrange("p a b -> p (a b)"))),
                             (1, turned_copy(p1)),
                             (0, scaled(y8, "y", "yd", lambda t: dinv[:, bass.ds(t, 1)]))])
            root(2)
            a.wait_ge(dve_step, mark["ln2"])

            half = RELS // 2

            def d2_exp(s, k, r):
                a.wait_ge(d2["gate"], s + 1)
                at_least(a, d2["dve"], s - TILES + 1)
                a.activation(gate[:, k, 0, :], ps[2 + k % 2][:, 0:RELS], ACT.Exp, scale=-1.0).then_inc(d2["gexp"], 1)

            def d2_out(s, k, r):
                a.wait_ge(d2["gsig"], s + 1)
                a.wait_ge(d2["prod"], s + 1)
                slot_free(a, d2["stored"][k], r)
                for q in range(half):
                    ins = a.activation(rel_out[:, k, (half + q) * F:(half + q + 1) * F],
                                       ps[5 + 2 * (k % 2)][:, q * F:(q + 1) * F], ACT.Copy,
                                       scale=gate[:, k, 0, half + q:half + q + 1])
                ins.then_inc(d2["act"], 1)

            staged(a, NODE_TILES, TILES, [(3, normed(d2)), (1, d2_exp), (0, d2_out)])
            pass_rows(gr2, 2, F)
            root(3)
            a.wait_ge(dve_step, mark["ln3"])

            def d3_out(s, k, r):
                a.wait_ge(d3["prod"], s + 1)
                slot_free(a, d3["stored"][k], r)
                a.activation(rel_out[:, k, half * F:RELS * F], ps[5 + 2 * (k % 2)][:], ACT.Copy).then_inc(d3["act"], 1)

            staged(a, NODE_TILES, TILES, [(3, normed(d3)), (0, d3_out)])
            pass_rows(gr3, 2, F)

        @block.tensor
        def _(t):
            win_regs = [t.alloc_register(f"pwin{k}") for k in range(XB * VSLOTS)]

            def windows(s, n):
                t.reg_load(win_regs[0:n], win[0:1, bass.ds(s, n)])
                return [t.snap(r, min_val=0, max_val=NODE_TILES - 1) for r in win_regs[0:n]]

            t.wait_ge(dve_step, mark["rows"])
            t.wait_ge(s_edges, 12 * 16)
            for c in range(CHUNKS):
                n = P if c < CHUNKS - 1 else CTAIL
                for kind in range(4):
                    ins = t.transpose(ps[c][:, kind * P:kind * P + n], R[0:n, c, kind, :], ident[0:n, 0:n])
                ins.then_inc(pe_prep, 1)
            t.wait_ge(s_extra, 16)
            for kind in range(4):
                ins = t.transpose(ps[CHUNKS][:, kind * P:kind * P + EXTRA], xrows[0:EXTRA, kind * P:(kind + 1) * P],
                                  ident[0:EXTRA, 0:EXTRA])
            ins.then_inc(pe_prep, 1)
            t.wait_ge(s_w, 16 * 9)
            t.wait_ge(dve_step, mark["wsum"])
            for j in range(4):
                t.transpose(ps[0][:, j * F:(j + 1) * F], wraw[:, j, :], ident[:])
            t.transpose(ps[1][:, 0:F], hs[:, 0, :], ident[:]).then_inc(pe_prep, 1)

            def turn(d, source, copied, banks):
                def body(s, k, r):
                    t.wait_ge(d[source], s + 1)
                    at_least(t, d[copied], s - len(banks) + 1)
                    t.transpose(ps[banks[k % len(banks)]][:, 0:F], hs[:, k, :], ident[:]).then_inc(d["turned"], 1)
                return body

            t.wait_ge(dve_step, mark["weights"])

            def d0_prod(s, k, r):
                t.wait_ge(d0["hT"], s + 1)
                at_least(t, d0["qv"], s - 1)
                at_least(t, d0["k"], s - 1)
                t.matmul(ps[2 + k % 2][:, 0:2 * F], hT[:, k, :], wqkvT[:, 0:2 * F], start=True, stop=True)
                t.matmul(ps[4 + k % 2][:, 0:F], hT[:, k, :], wqkvT[:, 2 * F:3 * F], start=True, stop=True).then_inc(d0["prod"], 1)

            staged(t, NODE_TILES, TILES, [(2, turn(d0, "h", "hT", D0_BANKS)), (0, d0_prod)])

            t.wait_ge(d0["k"], NODE_TILES)
            t.wait_ge(d0["qv"], NODE_TILES)
            t.wait_ge(s_scratch, 16 * 10)

            def q0_pass(count, base, setups):
                def turn_rows(s, k, r):
                    if base:
                        hot = onehot_x0[:, s, :]
                    else:
                        t.wait_ge(q0["onehot"], s + 1)
                        hot = onehot[:, k, :]
                    reuse(t, q0["copied"], s, BANKS, base)
                    t.transpose(ps[k % BANKS][:, 0:P], hot, ident[:]).then_inc(q0["turned"], 1)

                def expand(s, k, r, *w):
                    t.wait_ge(q0["copied"], s + (base + 1))
                    reuse(t, q0["prod"], s, BANKS, base)
                    t.matmul(ps[4 + k % BANKS][:, 0:F], onehotT[:, k % BANKS, :],
                             K[:, bass.ds(w[0] if w else s + 1, 1), :].rearrange("p a f -> p (a f)"),
                             start=True, stop=True).then_inc(q0["kexp"], 1)

                staged(t, count, EXTRA if base else RING, [(3, turn_rows), (0, expand)], setups)

            q0_pass(EDGE_TILES, 0, {0: windows})
            t.wait_ge(s_extra_hot, EXTRA)
            q0_pass(EXTRA, EDGE_TILES, {})

            t.wait_ge(dve_step, mark["blocks"])
            for b in range(0, BLOCKS, 4):
                at_least(t, s_mid_cp, b // 4 - 1)
                for j in range(min(4, BLOCKS - b)):
                    ins = t.transpose(ps[(b // 4) % 2][:, j * P:(j + 1) * P], FT[:, (b + j) * P:(b + j + 1) * P], ident[:])
                ins.then_inc(s_mid_pe, 1)
            for name, bank in (("f", 2), ("b", 4)):
                t.wait_ge(dve_step, mark["carry_" + name])
                t.transpose(ps[bank][0:1, 0:P], carry[:, 0:1], ident[:])
                t.transpose(ps[bank][0:1, P:2 * P], carry[:, 1:2], ident[:]).then_inc(s_mid_pe, 1)
                t.wait_ge(dve_step, mark["crow_" + name])
                o = 0 if name == "f" else 1
                t.matmul(ps[bank + 1][:, 0:1], crow[0:1, 2, o:o + P], one[0:1, 0:1], start=True, stop=True).then_inc(s_mid_pe, 1)
            t.wait_ge(act_step, 2)
            for b in range(0, BLOCKS, 4):
                at_least(t, s_mid_cp, MID + b // 4 - 3)
                for j in range(min(4, BLOCKS - b)):
                    ins = t.transpose(ps[(b // 4) % 4][:, j * P:(j + 1) * P], ST[:, (b + j) * P:(b + j + 1) * P], ident[:])
                ins.then_inc(s_mid_pe, 1)

            def a0_step(s, k, r):
                batch = k // VB + 1 + r * VSLOTS
                t.wait_ge(a0["onehot"] if k % VB < 2 else a0["onehot_act"], batch)
                t.wait_ge(a0["vw"], batch)
                t.wait_ge(a0["wcol"], batch)
                at_least(t, a0["added"], s - RING + 1)
                t.matmul(ps[k % RING][:, 0:ACCW], onehot_v[:, k, :], vw[:, k, :], start=True, stop=True).then_inc(a0["summed"], 1)

            def extra_products(g, width, hot, rows_of, setups, before=None):
                def body(b, _, r, *at):
                    if before:
                        before(b)
                    reuse(t, g["added"], b, VSLOTS, EDGE_TILES)
                    for i in range(XB):
                        t.matmul(ps[b % VSLOTS][:, i * width:(i + 1) * width], hot[:, b * XB + i, :],
                                 rows_of(i, b % VSLOTS, *at), start=True, stop=True).then_inc(g["summed"], 1)
                staged(t, XBATCH, XBATCH, [(0, body)], setups, group=VSLOTS)

            def weighed(b):
                t.wait_ge(a0["vw"], b + (MBATCH + 1))
                t.wait_ge(a0["wcol"], b + (MBATCH + 1))

            t.wait_ge(s_mid_cp, 2 * MID)
            staged(t, EDGE_TILES, VRING, [(0, a0_step)])
            extra_products(a0, ACCW, onehot_x0, lambda i, j: vw[:, j * VB + i, :], {}, weighed)

            def node_product(p, weight, free):
                def turn_batch(b, k, r, n):
                    t.wait_ge(p["inn"], b + 1)
                    at_least(t, p["T"], b - 1)
                    for i in range(n):
                        ins = t.transpose(ps[k][:, i * F:(i + 1) * F], hs8[:, k, i, :], ident[:])
                    ins.then_inc(p["turned"], 1)

                def product(b, k, r, n):
                    t.wait_ge(p["T"], b + 1)
                    at_least(t, free, b - 1)
                    for i in range(n):
                        ins = t.matmul(ps[4 + k][:, i * F:(i + 1) * F], hT8[:, k, i, :], weight, start=True, stop=True)
                    ins.then_inc(p["prod"], 1)

                tile_batches(t, [(1, turn_batch), (0, product)])

            t.wait_ge(a0["added"], EDGE_TILES + XBATCH)
            node_product(p0, wsT[:], p0["x"])

            def kept(b, n):
                regs = win_regs[0:n * XB]
                t.reg_load(regs, tile[0:1, 1, bass.ds(b * XB, n * XB)])
                at = [t.snap(r, min_val=0, max_val=NODE_TILES - 1) for r in regs]
                return [at[i * XB:(i + 1) * XB] for i in range(n)]

            def sum_pass(g, hot, width):
                def gathered(s, k, r):
                    t.wait_ge(g["onehot"], s + 1)
                    t.wait_ge(g["rows"][k], 16 * (r + 1))
                    at_least(t, g["added"], s - RING + 1)
                    t.matmul(ps[k][:, 0:width], onehot[:, k, :], ring[:, k, 0:width], start=True, stop=True).then_inc(g["summed"], 1)

                staged(t, EDGE_TILES, RING, [(0, gathered)])
                t.wait_ge(g["kept"], EDGE_TILES)
                t.wait_ge(s_extra_hot, hot)
                extra_products(g, width, onehot_x, lambda i, j, at: keep_g[:, bass.ds(at[i], 1), 0:width].rearrange(
                    "p a f -> p (a f)"), {0: kept})

            t.wait_ge(p0["x"], BATCHES)
            sum_pass(g1, EXTRA + 1, F + 1)
            t.wait_ge(g1["added"], EDGE_TILES + XBATCH)
            node_product(p1, w1T[:], p1["y"])

            def relations(d, w, gated):
                half = RELS // 2

                def gates(s, k, r):
                    t.wait_ge(d["hT"], s + 1)
                    at_least(t, d["gexp"], s - 1)
                    t.matmul(ps[2 + k % 2][:, 0:RELS], hT[:, k, :], g2[:], start=True, stop=True).then_inc(d["gate"], 1)

                def body(s, k, r):
                    t.wait_ge(d["hT"], s + 1)
                    at_least(t, d["dve"], s - 1)
                    at_least(t, d["act"], s - 1)
                    b = 4 + 2 * (k % 2)
                    t.matmul(ps[b][:], hT[:, k, :], w[:, 0:half, :].rearrange("p q f -> p (q f)"), start=True, stop=True)
                    t.matmul(ps[b + 1][:], hT[:, k, :], w[:, half:RELS, :].rearrange("p q f -> p (q f)"),
                             start=True, stop=True).then_inc(d["prod"], 1)

                staged(t, NODE_TILES, TILES, [(2, turn(d, "h", "hT", (0, 1)))] + [(1, gates)] * gated + [(0, body)])

            t.wait_ge(p1["y"], BATCHES)
            relations(d2, w2, True)
            t.wait_ge(d2["dve"], NODE_TILES)
            t.wait_ge(d2["act"], NODE_TILES)
            sum_pass(gr2, 2 * EXTRA + 1, F)
            t.wait_ge(gr2["added"], EDGE_TILES + XBATCH)
            relations(d3, w3, False)
            t.wait_ge(d3["dve"], NODE_TILES)
            t.wait_ge(d3["act"], NODE_TILES)
            sum_pass(gr3, 3 * EXTRA + 1, F)

        @block.sync
        def _(sp):
            full = (NODE_TILES - 1) * P
            sp.wait_ge(s_const, 1)
            c6 = (CHUNKS - 1) * P * P
            tail = (REAL_TILES - 1) * P
            for kind, a in ((0, dst), (1, src), (2, rel), (3, weight1)):
                t_ = R[:, :, 3, :] if kind == 3 else RI[:, :, kind, :]
                sp.dma_start(t_[:, 0:CHUNKS - 1, :], a[0:c6].rearrange("(c p i) -> p c i", p=P, i=P)).then_inc(s_edges, 16)
                sp.dma_start(t_[0:REAL_CTAIL - 1, CHUNKS - 1, :], a[c6:tail].rearrange("(p i) -> p i", i=P)).then_inc(s_edges, 16)
                sp.dma_start(t_[REAL_CTAIL - 1:REAL_CTAIL, CHUNKS - 1, 0:ETAIL], a[tail:E].rearrange("(a i) -> a i", a=1)).then_inc(s_edges, 16)
            sp.dma_start(X[:, 0:NODE_TILES - 1, :], x[0:full, :].rearrange("(t p) f -> p t f", p=P)).then_inc(s_x, 16)
            sp.dma_start(X[0:NTAIL, NODE_TILES - 1, :], x[full:N, :]).then_inc(s_x, 16)
            for j, w in enumerate((Wq, Wk, Wv, W1)):
                sp.dma_start(wraw[:, j, :], w).then_inc(s_w, 16)
            sp.dma_start(wsraw[:], Wscale.rearrange("(h i) c -> i h c", h=HEADS)).then_inc(s_w, 16)
            sp.dma_start(w2[:], W2.rearrange("r d f -> d r f")).then_inc(s_w, 16)
            sp.dma_start(w3[:], W3.rearrange("r d f -> d r f")).then_inc(s_w, 16)
            sp.dma_start(g2[:], gate2.rearrange("r d o -> d (r o)"), allow_slow_non_contiguous=True).then_inc(s_w, 16)
            sp.dma_start(bias[:], bass.AP(b1.tensor, 0, [[0, P], [1, F]])).then_inc(s_w, 16)

            sp.wait_ge(dve_step, mark["rows"])
            sp.wait_ge(s_const, 2)
            nfull = (CHUNKS - 1) * P
            sp.dma_start(win_d[1:1 + nfull].rearrange("(c p) -> p c", p=P), ends[:, 0:CHUNKS - 1], allow_slow_non_contiguous=True).then_inc(s_scratch, 16)
            sp.dma_start(win_d[1 + nfull:EDGE_TILES + 1].rearrange("(p a) -> p a", a=1),
                         ends[0:CTAIL, CHUNKS - 1:CHUNKS]).then_inc(s_scratch, 16)
            sp.dma_start(win_d[0:1].rearrange("(a b) -> a b", a=1), minus1[:, 2:3]).then_inc(s_scratch, 16)
            sp.dma_start(rows_d[0:nfull, :].rearrange("(c p) f -> p c f", p=P),
                         R[:, 0:CHUNKS - 1].rearrange("p c k i -> p c (k i)")).then_inc(s_scratch, 16)
            sp.dma_start(rows_d[nfull:EDGE_TILES, :], R[0:CTAIL, CHUNKS - 1].rearrange("p k i -> p (k i)")).then_inc(s_scratch, 16)
            sp.dma_start(dst_d[1:1 + nfull * P].rearrange("(c p i) -> p c i", p=P, i=P), RI[:, 0:CHUNKS - 1, 0, :]).then_inc(s_dst, 16)
            rest = GROUPS * BLOCKS - nfull
            sp.dma_start(dst_d[1 + nfull * P:1 + GROUPS * ROW].rearrange("(p i) -> p i", i=P), RI[0:rest, CHUNKS - 1, 0, :]).then_inc(s_dst, 16)
            sp.dma_start(dst_d[0:1].rearrange("(a b) -> a b", a=1), minus1[:, 0:1]).then_inc(s_dst, 16)
            sp.dma_start(dst_d[GROUPS * ROW + 1:GROUPS * ROW + 2].rearrange("(a b) -> a b", a=1), minus1[:, 1:2]).then_inc(s_dst, 16)
            sp.wait_ge(s_scratch, 16 * 5)
            sp.dma_start(winb_i, bass.AP(win_d.tensor, 0, [[0, P], [1, EDGE_TILES + 1]])).then_inc(s_scratch, 16)
            sp.dma_start(win[:], win_d[0:EDGE_TILES].rearrange("(a b) -> a b", a=1)).then_inc(s_scratch, 16)
            sp.wait_ge(dve_step, mark["tiles"])
            sp.wait_ge(s_scratch, 16 * 7)
            for j in range(2):
                sp.dma_start(tile_d[j].rearrange("(p a) -> p a", a=1), few[0:EXTRA, j:j + 1]).then_inc(s_scratch, 16)
            sp.wait_ge(s_scratch, 16 * 9)
            sp.dma_start(tile[:], tile_d.rearrange("(a k) b -> a k b", a=1)).then_inc(s_scratch, 16)
            sp.wait_ge(s_dst, 64)
            sp.wait_ge(dve_step, mark["cols"])
            for h in range(HEADS):
                sp.dma_start(drow[h * GROUPS:(h + 1) * GROUPS, :],
                             bass.AP(dst_d.tensor, 0, [[ROW, GROUPS], [1, ROW + 2]])).then_inc(s_dst, 16)

            def store(d, table, staged_rows, waits):
                def body(s, k, r):
                    for w in waits:
                        sp.wait_ge(w, s + 1)
                    sp.dma_start(table[bass.ds(s * P, P), :], staged_rows[:, k, :]).then_inc(d["stored"][k], 16)
                staged(sp, NODE_TILES, TILES, [(0, body)])

            store(d0, qv_d, qv_out, [d0["qv"]])

            def save(s, k, r):
                sp.wait_ge(q0["rows"][k], 16 * (r + 1))
                sp.dma_start(v_d[:, bass.ds(s, 1), :], ring[:, k, F:2 * F].rearrange("p (a f) -> p a f", a=1)).then_inc(q0["saved"][k], 16)

            staged(sp, EDGE_TILES, RING, [(0, save)])
            for k in range(RING):
                sp.wait_ge(q0["saved"][k], 16 * (EDGE_TILES // RING))

            sp.wait_ge(q0["prod"], EDGE_TILES)
            sp.wait_ge(s_kept, EDGE_TILES)

            tile_regs = [sp.alloc_register(f"vtile{j}") for j in range(XB * VSLOTS)]

            def load(b, j, r):
                reuse(sp, a0["vw"], b, VSLOTS)
                sp.dma_start(vin[:, j * VB:(j + 1) * VB, :], v_d[:, bass.ds(b * VB, VB), :]).then_inc(a0["loaded"][j], 16)

            def edge_tiles(b, n):
                regs = tile_regs[0:n * XB]
                sp.reg_load(regs, tile[0:1, 0, bass.ds(b * XB, n * XB)])
                at = [sp.snap(r, min_val=0, max_val=EDGE_TILES - 1) for r in regs]
                return [at[i * XB:(i + 1) * XB] for i in range(n)]

            def load_extra(b, j, r, tiles):
                sp.wait_ge(a0["vw"], b + (MBATCH - VSLOTS + 1))
                for i, at in enumerate(tiles):
                    sp.dma_start(vin[:, j * VB + i:j * VB + i + 1, :], v_d[:, bass.ds(at, 1), :]).then_inc(a0["loaded"][j], 16)

            staged(sp, MBATCH, VSLOTS, [(0, load)])
            staged(sp, XBATCH, VSLOTS, [(0, load_extra)], {0: edge_tiles})

            t1 = t1_d.rearrange("(t p) f -> p t f", p=P)
            for n, (a, b) in enumerate(PARTS[H_PARTS:] + PARTS[:H_PARTS]):
                sp.wait_ge(s_t1, n + 1)
                sp.dma_start(t1[:, a:b, :], Tst[:, a:b, :]).then_inc(s_t1d, 16)
            store(d2, t2_d.rearrange("(n r) f -> n (r f)", r=RELS), rel_out, [d2["dve"], d2["act"]])
            store(d3, t3_d.rearrange("(n r) f -> n (r f)", r=RELS), rel_out, [d3["dve"], d3["act"]])
            tiles = out[0:full, :].rearrange("(t p) f -> p t f", p=P)
            cuts = [XBATCH // 2, 3 * XBATCH // 4, XBATCH]
            a = 0
            for b in cuts:
                sp.wait_ge(s_final, 1 + b)
                z = min(1 + b * XB, NODE_TILES - 1)
                sp.dma_start(tiles[:, a:z, :], X[:, a:z, :]).then_inc(s_out, 16)
                a = z
            sp.dma_start(out[full:N, :], X[0:NTAIL, NODE_TILES - 1, :]).then_inc(s_out, 16)
            sp.wait_ge(s_out, 16 * (len(cuts) + 1))


_INS = ["x", "src", "dst", "edge_type_8", "edge_weight1", "L0_gnn_Wq", "L0_gnn_Wk", "L0_gnn_Wv", "L0_gnn_Wscale",
        "L1_gnn_W1_w", "L1_gnn_W1_b", "L2_gnn_weight", "L2_gnn_gate_weight", "L3_gnn_W"]


def kernel(**inputs):
    import numpy as np
    import concourse.bacc as bacc
    from concourse.bass_utils import run_bass_kernel_spmd

    nc = bacc.Bacc("TRN2", target_bir_lowering=False, num_devices=1)
    arrays, args = {}, []
    for name in _INS:
        a = np.ascontiguousarray(inputs[name])
        if name == "edge_weight1":
            a = a.reshape(-1)
        arrays["in_" + name] = a
        args.append(nc.dram_tensor("in_" + name, a.shape, mybir.dt.from_np(a.dtype), kind="ExternalInput").ap())
    out = nc.dram_tensor("out", (N, F), F32, kind="ExternalOutput").ap()
    graph_layers(nc, *args, out)
    return run_bass_kernel_spmd(nc, [arrays], core_ids=[0]).results[0]["out"]
```
